# Optimizing a Trainium2 kernel written in Bass

```python
import numpy as np
import jax
import jax.numpy as jnp

def _softmax(x, axis=-1):
    return jax.nn.softmax(x, axis=axis)

def _gelu(x):
    return jax.nn.gelu(x, approximate=True)

def _silu(x):
    return jax.nn.silu(x)

def _sigmoid(x):
    return jax.nn.sigmoid(x)

def _layernorm(x, axis=-1, eps=1e-05):
    m = jnp.mean(x, axis=axis, keepdims=True)
    v = jnp.var(x, axis=axis, keepdims=True)
    return (x - m) / jnp.sqrt(v + eps)

def _scatter_add(tgt, idx, src, axis=0):
    return tgt.at[idx].add(src)

def _segment_sum(src, seg, n):
    return jax.ops.segment_sum(src, seg, n)
kernel_name = 'mk_xattn_ffn_d2_seqx_r8_b1c17f'

def setup_inputs(seed: int=0):
    np.random.seed(seed)
    _w = jnp.asarray

    def _rec_inputs():
        import jax
        import jax.numpy as jnp
        _rk = jax.random.key(seed)
        x = -0.0002928 + 1 * jax.random.normal(jax.random.fold_in(_rk, 1), (32, 64, 128), jnp.float32)
        _lenS = 64 - jax.random.randint(jax.random.fold_in(_rk, 7), (32,), 0, max(1, 64 // 4) + 1, jnp.int32)
        _lenS2 = 64 - jax.random.randint(jax.random.fold_in(_rk, 8), (32,), 0, max(1, 64 // 4) + 1, jnp.int32)
        _ctx_1024P = jax.random.normal(jax.random.fold_in(_rk, 11), (32, 16, 128), jnp.float32)
        _ctx_1024c = jax.random.dirichlet(jax.random.fold_in(_rk, 511), 0.3 * jnp.ones((16,), jnp.float32), (32, 64))
        _ctx_1024t = jnp.einsum('bsk,bkd->bsd', _ctx_1024c, _ctx_1024P)
        _ctx_1024t = _ctx_1024t * jax.lax.rsqrt(jnp.mean(jnp.square(_ctx_1024t)) + 1e-12) * 0.953939
        ctx_1024 = -1.39393e-06 + 0.999914 * (_ctx_1024t + 0.3 * jax.random.normal(jax.random.fold_in(_rk, 611), (32, 64, 128), jnp.float32))
        return (x, ctx_1024)
    x, ctx_1024 = _rec_inputs()

    def _L0_xattn_setup():
        import jax, jax.numpy as jnp
        import numpy as np
        K_DIM = 128
        HEADS = 16
        key = jax.random.key(seed)
        ks = jax.random.split(key, 8)
        b, t, tc, k = (2, 256, 256, K_DIM)
        scale = 1.0 / np.sqrt(k)
        x = jax.random.normal(ks[0], (b, t, k), dtype=jnp.float32)
        context = jax.random.normal(ks[1], (b, tc, k), dtype=jnp.float32)
        Wq = jax.random.normal(ks[2], (k, k), dtype=jnp.float32) * scale
        Wk = jax.random.normal(ks[3], (k, k), dtype=jnp.float32) * scale
        Wv = jax.random.normal(ks[4], (k, k), dtype=jnp.float32) * scale
        Wo = jax.random.normal(ks[5], (k, k), dtype=jnp.float32) * scale
        bo = jax.random.normal(ks[6], (k,), dtype=jnp.float32) * 0.01
        return {'x': x, 'context': context, 'Wq': Wq, 'Wk': Wk, 'Wv': Wv, 'Wo': Wo, 'bo': bo}
    _L0_xattn_all = _L0_xattn_setup()
    _L0_xattn_in = {k: v for k, v in _L0_xattn_all.items() if k in ('Wq', 'Wk', 'Wv', 'Wo', 'bo')}
    del _L0_xattn_all

    def _L0_ffn_setup():
        import jax, jax.numpy as jnp
        import numpy as np
        TOP_K = 2
        EPS = 1e-09
        key = jax.random.key(seed)
        ks = jax.random.split(key, 6)
        B, T, D, H, E = (4, 256, 128, 256, 8)
        x = jax.random.normal(ks[0], (B, T, D), dtype=jnp.float32)
        Wg = jax.random.normal(ks[1], (E, D), dtype=jnp.float32) * 0.02
        W1 = jax.random.normal(ks[2], (E, 2 * H, D), dtype=jnp.float32) * 0.02
        b1 = jax.random.normal(ks[3], (E, 2 * H), dtype=jnp.float32) * 0.02
        Wo = jax.random.normal(ks[4], (D, H), dtype=jnp.float32) * 0.02
        bo = jax.random.normal(ks[5], (D,), dtype=jnp.float32) * 0.02
        return {'x': x, 'Wg': Wg, 'W1': W1, 'b1': b1, 'Wo': Wo, 'bo': bo}
    _L0_ffn_all = _L0_ffn_setup()
    _L0_ffn_in = {k: v for k, v in _L0_ffn_all.items() if k in ('Wg', 'W1', 'b1', 'Wo', 'bo')}
    del _L0_ffn_all

    def _L1_xattn_setup():
        import jax, jax.numpy as jnp
        import numpy as np
        B, L, D = (8, 256, 128)
        key = jax.random.key(seed)
        k1, k2, k3 = jax.random.split(key, 3)
        enc_outputs = jax.random.normal(k1, (B, L, D), dtype=jnp.float32)
        x = jax.random.normal(k2, (B, L, D), dtype=jnp.float32)
        Wq = jax.random.normal(k3, (D, D), dtype=jnp.float32) * (1.0 / np.sqrt(D))
        return {'enc_outputs': enc_outputs, 'x': x, 'Wq': Wq}
    _L1_xattn_all = _L1_xattn_setup()
    _L1_xattn_in = {k: v for k, v in _L1_xattn_all.items() if k in ('Wq',)}
    del _L1_xattn_all

    def _L1_ffn_setup():
        import jax, jax.numpy as jnp
        import numpy as np
        DIM = 128

        def _reference_tuple_inner(x, W_r, W_k, W_v, mu_r, mu_k):
            B, T, C = x.shape
            x_prev = jnp.concatenate([jnp.zeros((B, 1, C), x.dtype), x[:, :-1, :]], axis=1)
            xr = mu_r * x + (1.0 - mu_r) * x_prev
            xk = mu_k * x + (1.0 - mu_k) * x_prev
            r = jax.nn.sigmoid(jnp.einsum('btc,dc->btd', xr, W_r))
            k = jnp.einsum('btc,dc->btd', xk, W_k)
            k_act = jnp.square(jax.nn.relu(k))
            out = r * jnp.einsum('btc,dc->btd', k_act, W_v)
            new_state = x[:, -1, :]
            return (out, new_state)
        key = jax.random.key(seed)
        ks = jax.random.split(key, 6)
        B, T, C = (8, 256, DIM)
        x = jax.random.normal(ks[0], (B, T, C), dtype=jnp.float32)
        s = 1.0 / np.sqrt(C)
        W_r = jax.random.uniform(ks[1], (C, C), jnp.float32, -s, s)
        W_k = jax.random.uniform(ks[2], (C, C), jnp.float32, -s, s)
        W_v = jax.random.uniform(ks[3], (C, C), jnp.float32, -s, s)
        mu_r = jax.random.uniform(ks[4], (C,), jnp.float32)
        mu_k = jax.random.uniform(ks[5], (C,), jnp.float32)
        return {'x': x, 'W_r': W_r, 'W_k': W_k, 'W_v': W_v, 'mu_r': mu_r, 'mu_k': mu_k}
    _L1_ffn_all = _L1_ffn_setup()
    _L1_ffn_in = {k: v for k, v in _L1_ffn_all.items() if k in ('W_r', 'W_k', 'W_v', 'mu_r', 'mu_k')}
    del _L1_ffn_all
    return {'x': x, 'ctx_1024': ctx_1024, 'L0_xattn_Wq': _L0_xattn_in['Wq'], 'L0_xattn_Wk': _L0_xattn_in['Wk'], 'L0_xattn_Wv': _L0_xattn_in['Wv'], 'L0_xattn_Wo': _L0_xattn_in['Wo'], 'L0_xattn_bo': _L0_xattn_in['bo'], 'L0_ffn_Wg': _L0_ffn_in['Wg'], 'L0_ffn_W1': _L0_ffn_in['W1'], 'L0_ffn_b1': _L0_ffn_in['b1'], 'L0_ffn_Wo': _L0_ffn_in['Wo'], 'L0_ffn_bo': _L0_ffn_in['bo'], 'L1_xattn_Wq': _L1_xattn_in['Wq'], 'L1_ffn_W_r': _L1_ffn_in['W_r'], 'L1_ffn_W_k': _L1_ffn_in['W_k'], 'L1_ffn_W_v': _L1_ffn_in['W_v'], 'L1_ffn_mu_r': _L1_ffn_in['mu_r'], 'L1_ffn_mu_k': _L1_ffn_in['mu_k']}

def reference(x, ctx_1024, L0_xattn_Wq, L0_xattn_Wk, L0_xattn_Wv, L0_xattn_Wo, L0_xattn_bo, L0_ffn_Wg, L0_ffn_W1, L0_ffn_b1, L0_ffn_Wo, L0_ffn_bo, L1_xattn_Wq, L1_ffn_W_r, L1_ffn_W_k, L1_ffn_W_v, L1_ffn_mu_r, L1_ffn_mu_k):
    import jax
    import jax.numpy as jnp

    def _L0_xattn_ref(x, context, Wq, Wk, Wv, Wo, bo):
        import jax, jax.numpy as jnp
        import numpy as np
        K_DIM = 128
        HEADS = 16
        b, t, e = x.shape
        tc = context.shape[1]
        h = HEADS
        s = e // h
        q = (x @ Wq.T).reshape(b, t, h, s)
        k_ = (context @ Wk.T).reshape(b, tc, h, s)
        v = (context @ Wv.T).reshape(b, tc, h, s)
        inv4 = e ** (-0.25)
        q = q * inv4
        k_ = k_ * inv4
        dot = jnp.einsum('bthd,bchd->bhtc', q, k_)
        attn = jax.nn.softmax(dot, axis=-1)
        out = jnp.einsum('bhtc,bchd->bthd', attn, v).reshape(b, t, e)
        return out @ Wo.T + bo

    def _L0_ffn_ref(x, Wg, W1, b1, Wo, bo):
        import jax, jax.numpy as jnp
        import numpy as np
        TOP_K = 2
        EPS = 1e-09
        E = Wg.shape[0]
        gate_logits = jnp.einsum('btd,ed->bte', x, Wg)
        gate_scores = jax.nn.softmax(gate_logits, axis=-1)
        topk_val, topk_idx = jax.lax.top_k(gate_scores, TOP_K)
        topk_val = topk_val / (topk_val.sum(axis=-1, keepdims=True) + EPS)
        comb = (jax.nn.one_hot(topk_idx, E, dtype=x.dtype) * topk_val[..., None]).sum(axis=-2)
        out = jnp.zeros_like(x)
        for e in range(E):
            h = jnp.einsum('btd,hd->bth', x, W1[e]) + b1[e]
            a, b = jnp.split(h, 2, axis=-1)
            g = a * jax.nn.sigmoid(b)
            eo = jnp.einsum('bth,dh->btd', g, Wo) + bo
            out = out + eo * comb[..., e:e + 1]
        return out

    def _L1_xattn_ref(enc_outputs, x, Wq):
        import jax, jax.numpy as jnp
        import numpy as np
        B, L, D = (8, 256, 128)
        d_k = x.shape[-1]
        q = jnp.einsum('bld,hd->blh', x, Wq)
        k = jnp.einsum('bld,hd->blh', enc_outputs, Wq)
        v = k
        scores = jnp.einsum('bqh,bkh->bqk', q, k) / jnp.sqrt(jnp.float32(d_k))
        Lq, Lk = (scores.shape[1], scores.shape[2])
        causal = jnp.tril(jnp.ones((Lq, Lk), dtype=bool))
        scores = jnp.where(causal, scores, -jnp.inf)
        attn = jax.nn.softmax(scores, axis=-1)
        return jnp.einsum('bqk,bkh->bqh', attn, v)

    def _L1_ffn_ref(x, W_r, W_k, W_v, mu_r, mu_k):
        import jax, jax.numpy as jnp
        import numpy as np
        DIM = 128

        def _reference_tuple_inner(x, W_r, W_k, W_v, mu_r, mu_k):
            B, T, C = x.shape
            x_prev = jnp.concatenate([jnp.zeros((B, 1, C), x.dtype), x[:, :-1, :]], axis=1)
            xr = mu_r * x + (1.0 - mu_r) * x_prev
            xk = mu_k * x + (1.0 - mu_k) * x_prev
            r = jax.nn.sigmoid(jnp.einsum('btc,dc->btd', xr, W_r))
            k = jnp.einsum('btc,dc->btd', xk, W_k)
            k_act = jnp.square(jax.nn.relu(k))
            out = r * jnp.einsum('btc,dc->btd', k_act, W_v)
            new_state = x[:, -1, :]
            return (out, new_state)
        return _reference_tuple_inner(x, W_r, W_k, W_v, mu_r, mu_k)[0]
    x = x + _L0_xattn_ref(_layernorm(x, axis=-1), ctx_1024, L0_xattn_Wq, L0_xattn_Wk, L0_xattn_Wv, L0_xattn_Wo, L0_xattn_bo)
    x = x + _L0_ffn_ref(_layernorm(x, axis=-1), L0_ffn_Wg, L0_ffn_W1, L0_ffn_b1, L0_ffn_Wo, L0_ffn_bo)
    x = x + _L1_xattn_ref(ctx_1024, _layernorm(x, axis=-1), L1_xattn_Wq)
    x = x + _L1_ffn_ref(_layernorm(x, axis=-1), L1_ffn_W_r, L1_ffn_W_k, L1_ffn_W_v, L1_ffn_mu_r, L1_ffn_mu_k)
    return x

_drawn_inputs = setup_inputs


def setup_inputs(seed=0):
    import zlib

    import numpy as np

    out = dict(_drawn_inputs(seed))
    spreads = {}
    factors = {'L0_xattn_bo': 6.261,
     'L0_ffn_Wg': 3.0,
     'L0_ffn_W1': 2.692,
     'L0_ffn_b1': 26.978,
     'L0_ffn_bo': 2.907,
     'L1_ffn_W_r': 3.417,
     'L1_ffn_mu_r': 8.0}
    for name, (base, spread) in spreads.items():
        noise = np.random.default_rng([zlib.crc32(name.encode()), seed]).standard_normal(out[name].shape)
        drawn = base * np.exp(spread * noise) if base else spread * noise
        out[name] = jnp.asarray(drawn.astype(out[name].dtype))
    for name, factor in factors.items():
        out[name] = (out[name] * factor).astype(out[name].dtype)
    return out
```

```python
import concourse.bass as bass
from concourse import mybir
from contextlib import ExitStack

F32 = mybir.dt.float32
F16 = mybir.dt.float16
U32 = mybir.dt.uint32
ALU = mybir.AluOpType
ACT = mybir.ActivationFunctionType
AX = mybir.AxisListType

P = 128
BATCH, SEQ, D = 32, 64, 128
HEADS = 16
HD = D // HEADS
PAIRS = HEADS // 2
ROWG = 4
HPG = HEADS // ROWG
EXPERTS, HID = 8, 256
UP = 2 * HID
TILES = 4
BPG = 2 * TILES
TOK = TILES * P
GROUPS = BATCH * SEQ // TOK
RING = 6
GBUF = 4
POOL_E = 6
EPS_LN = 1e-5
EPS_GATE = 1e-9
SCALE0 = float(D) ** -0.5
SCALE1 = float(D) ** -0.5
NEG = -1e30
SETTLES = 33


def spread(ap, axis, n):
    shape = list(ap.shape)
    assert shape[axis] == 1
    shape[axis] = n
    return ap.broadcast_to(shape)


def build(nc, x, ctx_1024, L0_xattn_Wq, L0_xattn_Wk, L0_xattn_Wv, L0_xattn_Wo, L0_xattn_bo,
          L0_ffn_Wg, L0_ffn_W1, L0_ffn_b1, L0_ffn_Wo, L0_ffn_bo, L1_xattn_Wq,
          L1_ffn_W_r, L1_ffn_W_k, L1_ffn_W_v, L1_ffn_mu_r, L1_ffn_mu_k, out):
    x_dram = x.rearrange("b s d -> (b s) d").rearrange("(n p) d -> p n d", p=P)
    ctx_dram = ctx_1024.rearrange("b s d -> (b s) d").rearrange("(n p) d -> p n d", p=P)
    out_dram = out.rearrange("b s d -> (b s) d").rearrange("(n p) d -> p n d", p=P)

    with ExitStack() as stack:
        def sb(name, shape, dt=F32):
            return stack.enter_context(nc.sbuf_tensor(name, shape, dt))

        def sem(name):
            return stack.enter_context(nc.semaphore(name))

        SQ = 8
        WQ0, WK0, WV0, WO0, WQ1, WR, WKF, WVF = range(SQ)
        w_nat = sb("w_nat", [P, SQ, D])
        w1_nat = sb("w1_nat", [P, EXPERTS * UP // P, D])
        wof_nat = sb("wof_nat", [P, 2, P])
        wg_nat = sb("wg_nat", [EXPERTS, D])
        b1_nat = sb("b1_nat", [EXPERTS * UP // P, P])
        bo0 = sb("bo0", [P, D])
        bof = sb("bof", [P, D])
        mu = sb("mu", [P, 2])
        wT = sb("wT", [P, SQ, D])
        wmix = sb("wmix", [P, 2, 2, D])
        omu = sb("omu", [P, 2])
        w1h = sb("w1h", [P, EXPERTS, UP], F16)
        w1l = sb("w1l", [P, EXPERTS, UP], F16)
        wofT = sb("wofT", [P, 2, D])
        wgh = sb("wgh", [P, EXPERTS], F16)
        wgl = sb("wgl", [P, EXPERTS], F16)
        ident = sb("ident", [P, P])
        headmask = sb("headmask", [P, HPG, SEQ])
        causal = sb("causal", [P, P])
        hm0 = sb("hm0", [P, 3, HPG])
        hm1 = sb("hm1", [P, ROWG, HPG])
        iota_e = sb("iota_e", [P, EXPERTS])
        iota_i = sb("iota_i", [P, EXPERTS], mybir.dt.int32)
        eps_t = sb("eps_t", [P, TILES])
        mhalf = sb("mhalf", [P, TILES])
        spare = sb("spare", [P, 1])
        xin = sb("xin", [P, TILES, D])
        cin = sb("cin", [P, TILES, D])
        xres = sb("xres", [P, TILES, D])
        xout = sb("xout", [P, TILES, D])
        xn = sb("xn", [P, TILES, D])
        stats = sb("stats", [P, TILES, 6])
        mv = sb("mv", [P, TILES, 2])
        vare = sb("vare", [P, TILES])
        rstd = sb("rstd", [P, TILES])
        xnT = sb("xnT", [P, TOK])
        ctxT = sb("ctxT", [P, TOK])
        ctx2 = sb("ctx2", [P, BPG, 2, SEQ])
        qm = sb("qm", [P, BPG, 2, 2, SEQ])
        kT = sb("kT", [P, TOK])
        kbd = sb("kbd", [P, BPG, HPG, SEQ])
        vxh = sb("vxh", [P, BPG, 2, 4, 2, HD + 1], F16)
        vxl = sb("vxl", [P, BPG, 2, 4, 2, HD + 1], F16)
        k1T = sb("k1T", [P, TOK])
        v1 = sb("v1", [P, TILES, D])
        mx = sb("mx", [P, 2, HEADS])
        ssub = sb("ssub", [P, 2, HEADS * SEQ])
        prob = sb("prob", [P, 2, HEADS * SEQ])
        ph = sb("ph", [P, 2, PAIRS, P], F16)
        pl = sb("pl", [P, 2, PAIRS, P], F16)
        rden = sb("rden", [P, HEADS])
        onorm = sb("onorm", [P, 2, D])
        oT = sb("oT", [P, 2, P])
        xh = sb("xh", [P, TOK], F16)
        xl = sb("xl", [P, TOK], F16)
        lg = sb("lg", [P, TILES, EXPERTS])
        top = sb("top", [P, TILES, 8])
        topi = sb("topi", [P, TILES, 8], U32)
        topf = sb("topf", [P, TILES, 2])
        ls = sb("ls", [P, TILES, EXPERTS])
        ge = sb("ge", [P, TILES, EXPERTS])
        sel0 = sb("sel0", [P, TILES, EXPERTS])
        sel1 = sb("sel1", [P, TILES, EXPERTS])
        es = sb("es", [P, TILES, EXPERTS])
        ssum = sb("ssum", [P, TILES])
        zsum = sb("zsum", [P, TILES])
        gden = sb("gden", [P, TILES])
        comb = sb("comb", [P, TILES, EXPERTS])
        csum = sb("csum", [P, TILES])
        sg = sb("sg", [P, RING, HID])
        gb = sb("gb", [P, GBUF, HID])
        accp = sb("accp", [P, 2, HID])
        accd = sb("accd", [P, 2, HID])
        g67 = sb("g67", [P, 2, HID])
        gT = sb("gT", [P, 2, 2, P])
        q1T = sb("q1T", [P, TOK])
        sm1 = sb("sm1", [P, TILES, P])
        mx1 = sb("mx1", [P, TILES])
        nb1 = sb("nb1", [P, TILES])
        den1 = sb("den1", [P, TILES])
        rd1 = sb("rd1", [P, TILES])
        p1 = sb("p1", [P, TILES, P])
        p1T = sb("p1T", [P, TILES, P])
        x4p = sb("x4p", [P, BPG, SEQ + 1])
        krelu = sb("krelu", [P, TOK])
        kact = sb("kact", [P, TOK])
        th = sb("th", [P, TOK])
        uu = sb("uu", [P, TOK])

        ps = stack.enter_context(nc.psum_tensor("ps", [P, 8, 512], F32))

        ld_sq = sem("ld_sq")
        ld_bo0 = sem("ld_bo0")
        ld_bof = sem("ld_bof")
        ld_wg = sem("ld_wg")
        ld_mu = sem("ld_mu")
        c_pow = sem("c_pow")
        c_hm = sem("c_hm")
        c_cau = sem("c_cau")
        c_iota = sem("c_iota")
        wmix_s = sem("wmix_s")
        wgl_s = sem("wgl_s")
        ld_w1 = sem("ld_w1")
        ld_wof = sem("ld_wof")
        ld_small = sem("ld_small")
        c_id0 = sem("c_id0")
        c_ident = sem("c_ident")
        c_const0 = sem("c_const0")
        c_const = sem("c_const")
        vx_clear = sem("vx_clear")
        vx_ones = sem("vx_ones")
        wt_ps = sem("wt_ps")
        wt_sb = sem("wt_sb")
        omu_s = sem("omu_s")
        b1_ps = sem("b1_ps")
        w1_sub = sem("w1_sub")
        w1_adj = sem("w1_adj")
        wg_adj = sem("wg_adj")
        w1_ps = sem("w1_ps")
        w1_hi = sem("w1_hi")
        w1_lo = sem("w1_lo")
        cin_in = sem("cin_in")
        xin_in = sem("xin_in")
        ctxT_ps = sem("ctxT_ps")
        ctxT_sb = sem("ctxT_sb")
        ctx2_sb = sem("ctx2_sb")
        kT_ps = sem("kT_ps")
        kT_sb = sem("kT_sb")
        v_ps = sem("v_ps")
        v_hi = sem("v_hi")
        v_lo = sem("v_lo")
        st = sem("st")
        ln_var = sem("ln_var")
        ln_ve = sem("ln_ve")
        ln_rstd = sem("ln_rstd")
        xn_sb = sem("xn_sb")
        xnT_ps = sem("xnT_ps")
        xnT_sb = sem("xnT_sb")
        xb_sb = sem("xb_sb")
        qT_ps = sem("qT_ps")
        qT_sb = sem("qT_sb")
        kbd_sb = sem("kbd_sb")
        k1_ps = sem("k1_ps")
        k1_sb = sem("k1_sb")
        v1_ps = sem("v1_ps")
        v1_sb = sem("v1_sb")
        s_ps = sem("s_ps")
        s_sub = sem("s_sub")
        p_sb = sem("p_sb")
        pT_ps = sem("pT_ps")
        p_hi = sem("p_hi")
        p_lo = sem("p_lo")
        o_ps = sem("o_ps")
        o_nrm = sem("o_nrm")
        oT_ps = sem("oT_ps")
        oT_sb = sem("oT_sb")
        y0_ps = sem("y0_ps")
        x1_sb = sem("x1_sb")
        xh_sb = sem("xh_sb")
        xl_sb = sem("xl_sb")
        lg_ps = sem("lg_ps")
        ls_sb = sem("ls_sb")
        ge_sb = sem("ge_sb")
        comb_sb = sem("comb_sb")
        h_ps = sem("h_ps")
        sg_sb = sem("sg_sb")
        g_sb = sem("g_sb")
        acc_pool = sem("acc_pool")
        acc_p1 = sem("acc_p1")
        acc_sb = sem("acc_sb")
        gT_ps = sem("gT_ps")
        gT_sb = sem("gT_sb")
        y1_ps = sem("y1_ps")
        x2_sb = sem("x2_sb")
        q1_ps = sem("q1_ps")
        q1_sb = sem("q1_sb")
        s1_ps = sem("s1_ps")
        nb1_sb = sem("nb1_sb")
        p1_sb = sem("p1_sb")
        p1T_ps = sem("p1T_ps")
        p1T_sb = sem("p1T_sb")
        y2_ps = sem("y2_ps")
        kf_ps = sem("kf_ps")
        kr_sb = sem("kr_sb")
        kact_sb = sem("kact_sb")
        r_ps = sem("r_ps")
        th_sb = sem("th_sb")
        vf_ps = sem("vf_ps")
        u_sb = sem("u_sb")
        uT_ps = sem("uT_ps")
        xo_sb = sem("xo_sb")
        xout_free = sem("xout_free")

        W1CH = EXPERTS * UP // P
        NWT = 3
        block = stack.enter_context(nc.Block())


        def v_src(half, m):
            v = ps[half, 2:4, :].rearrange("p a (b c) -> p (a b) c", c=SEQ)
            return v.rearrange("p n (h m d) -> p n h m d", m=2, d=HD)[:, :, :, m, :]

        def v_half(buf, half, m):
            return buf[half, :, :, :, m, 0:HD].rearrange("p b g h d -> p (b g) h d")

        def at(i, per, k):
            return i * per + k

        @block.sync
        def _(sp):
            squares = [L0_xattn_Wq, L0_xattn_Wk, L0_xattn_Wv, L0_xattn_Wo, L1_xattn_Wq,
                       L1_ffn_W_r, L1_ffn_W_k, L1_ffn_W_v]
            sp.dma_start(cin[:, :, :], ctx_dram[:, 0:TILES, :]).then_inc(cin_in, 16)
            sp.dma_start(xin[:, :, :], x_dram[:, 0:TILES, :]).then_inc(xin_in, 16)
            for n in range(SQ):
                sp.dma_start(w_nat[:, n, :], squares[n]).then_inc(ld_sq, 16)
            sp.dma_start(bo0[:, :], spread(L0_xattn_bo.rearrange("(a d) -> a d", a=1), 0, P)).then_inc(ld_bo0, 16)
            sp.dma_start(w1_nat[:, :, :], L0_ffn_W1.rearrange("e (j p) d -> p (e j) d", p=P)).then_inc(ld_w1, 16)
            with sp.Fori(1, GROUPS) as i:
                sp.wait_ge(ctxT_ps, i)
                sp.dma_start(cin[:, :, :], ctx_dram[:, bass.ts(i, TILES), :]).then_inc(cin_in, 16)
                sp.wait_ge(xn_sb, at(i, 4 * TILES, -3 * TILES))
                sp.wait_ge(xb_sb, i)
                sp.dma_start(xin[:, :, :], x_dram[:, bass.ts(i, TILES), :]).then_inc(xin_in, 16)
                sp.wait_ge(xo_sb, i)
                sp.dma_start(out_dram[:, bass.ds(i * TILES - TILES, TILES), :], xout[:, :, :]).then_inc(xout_free, 16)
            sp.wait_ge(xo_sb, GROUPS)
            sp.dma_start(out_dram[:, (GROUPS - 1) * TILES:GROUPS * TILES, :], xout[:, :, :]).then_inc(xout_free, 16)
            sp.wait_ge(xout_free, 16 * GROUPS + 16)

        @block.gpsimd
        def _(pool):
            pool.memset(ident[:, :], 0.0).then_inc(c_id0, 1)
            pool.wait_ge(c_id0, 1)
            pool.affine_select(out=ident[:, :], in_=ident[:, :], compare_op=ALU.not_equal, fill=1.0,
                               base=0, pattern=[[-1, P]], channel_multiplier=1).then_inc(c_ident, 1)
            pool.memset(eps_t[:, :], EPS_LN)
            pool.memset(mhalf[:, :], -0.5).then_inc(c_pow, 1)
            pool.memset(hm0[:, :, :], 0.0).then_inc(c_hm, 1)
            pool.wait_ge(c_hm, 1)
            pool.memset(hm1[:, :, :], 1.0).then_inc(c_hm, 1)
            pool.wait_ge(c_hm, 2)
            pool.affine_select(out=hm1[:, :, :], in_=hm1[:, :, :], compare_op=ALU.is_ge, fill=0.0,
                               base=0, pattern=[[-32, ROWG], [-HD, HPG]], channel_multiplier=1).then_inc(c_hm, 1)
            pool.wait_ge(c_hm, 3)
            pool.affine_select(out=hm1[:, :, :], in_=hm1[:, :, :], compare_op=ALU.is_ge, fill=0.0,
                               base=HD - 1, pattern=[[32, ROWG], [HD, HPG]], channel_multiplier=-1).then_inc(c_hm, 1)
            pool.wait_ge(c_hm, 4)
            pool.tensor_tensor(hm0[:, 0, :], hm1[:, 0, :], hm1[:, 1, :], ALU.add)
            pool.tensor_tensor(hm0[:, 1, :], hm1[:, 2, :], hm1[:, 3, :], ALU.add).then_inc(c_hm, 1)
            pool.wait_ge(c_hm, 5)
            pool.tensor_tensor(hm0[:, 2, :], hm0[:, 0, :], hm0[:, 1, :], ALU.add).then_inc(c_hm, 1)
            pool.wait_ge(c_hm, 6)
            pool.tensor_copy(headmask[:, :, :], spread(hm0[:, 2, :].unsqueeze(2), 2, SEQ)).then_inc(c_hm, 1)
            pool.wait_ge(c_hm, 7)
            pool.memset(causal[:, :], 0.0).then_inc(c_cau, 1)
            pool.wait_ge(c_cau, 1)
            pool.affine_select(out=causal[:, :], in_=causal[:, :], compare_op=ALU.is_ge, fill=NEG,
                               base=0, pattern=[[-1, P]], channel_multiplier=1).then_inc(c_cau, 1)
            pool.wait_ge(c_cau, 2)
            pool.memset(causal[SEQ:P, 0:SEQ], NEG).then_inc(c_cau, 1)
            pool.wait_ge(c_cau, 3)
            pool.iota(iota_i[:, :], [[1, EXPERTS]], base=0, channel_multiplier=0).then_inc(c_iota, 1)
            pool.wait_ge(c_iota, 1)
            pool.tensor_copy(iota_e[:, :], iota_i[:, :]).then_inc(c_iota, 1)

            with pool.Fori(0, GROUPS) as i:
                def rstd_of(n):
                    pool.wait_ge(ln_var, at(i, 4, n))
                    pool.tensor_tensor(vare[:, :], mv[:, :, 1], eps_t[:, :], ALU.add).then_inc(ln_ve, 1)
                    pool.wait_ge(ln_ve, at(i, 4, n))
                    pool.tensor_tensor(rstd[:, :], vare[:, :], mhalf[:, :], ALU.pow).then_inc(ln_rstd, 1)

                rstd_of(1)
                pool.wait_ge(xin_in, at(i, 16, 16))
                pool.wait_ge(ld_bo0, 16)
                pool.tensor_tensor(xres[:, :, :], xin[:, :, :], spread(bo0[:, :].unsqueeze(1), 1, TILES),
                                   ALU.add).then_inc(xb_sb, 1)
                pool.wait_ge(kT_sb, at(i, 1, 1))
                for b in range(BPG):
                    pool.tensor_tensor(kbd[:, b, :, :], spread(kT[:, bass.ts(b, SEQ)].unsqueeze(1), 1, HPG),
                                       headmask[:, :, :], ALU.mult).then_inc(kbd_sb, 1)
                rstd_of(2)
                for t in range(TILES):
                    for e in range(1, POOL_E):
                        n = t * POOL_E + e
                        pool.wait_ge(g_sb, at(i, TILES * EXPERTS, t * EXPERTS + e + 1))
                        if e == 1:
                            if t >= 2:
                                pool.wait_ge(acc_sb, at(i, TILES, t - 1))
                            pool.tensor_tensor(accp[:, t % 2, :], gb[:, (n - 1) % GBUF, :], gb[:, n % GBUF, :],
                                               ALU.add).then_inc(acc_pool, 1)
                        else:
                            pool.wait_ge(acc_pool, at(i, TILES * (POOL_E - 1), t * (POOL_E - 1) + e - 1))
                            pool.tensor_tensor(accp[:, t % 2, :], accp[:, t % 2, :], gb[:, n % GBUF, :],
                                               ALU.add).then_inc(acc_pool, 1)
                rstd_of(3)
                rstd_of(4)

        @block.scalar
        def _(act):
            act.dma_start(wof_nat[:, :, :], L0_ffn_Wo.rearrange("d (j p) -> d j p", p=P)).then_inc(ld_small, 16)
            act.dma_start(wg_nat[:, :], L0_ffn_Wg).then_inc(ld_wg, 16)
            act.dma_start(b1_nat[:, :], L0_ffn_b1.rearrange("e (j p) -> (e j) p", p=P)).then_inc(ld_small, 16)
            act.dma_start(bof[:, :], spread(L0_ffn_bo.rearrange("(a d) -> a d", a=1), 0, P)).then_inc(ld_bof, 16)
            act.dma_start(mu[:, 0:1], L1_ffn_mu_r.rearrange("(d a) -> d a", a=1)).then_inc(ld_mu, 16)
            act.dma_start(mu[:, 1:2], L1_ffn_mu_k.rearrange("(d a) -> d a", a=1)).then_inc(ld_mu, 16)
            for n in range(2):
                act.wait_ge(wt_ps, n + 1)
                act.activation(wT[:, 4 * n:4 * n + 4, :], ps[:, n, :], ACT.Copy).then_inc(wt_sb, 1)
            act.wait_ge(wt_ps, 3)
            act.activation(wofT[:, :, :], ps[:, 2, 0:2 * P], ACT.Copy)
            act.activation(wgh[:, :], ps[:, 2, 2 * P:2 * P + EXPERTS], ACT.Copy).then_inc(wt_sb, 1)
            for e in range(EXPERTS):
                act.wait_ge(w1_ps, e + 1)
                act.activation(w1h[:, e, :], ps[:, 4 + e % 4, :], ACT.Copy).then_inc(w1_hi, 1)

            with act.Fori(0, GROUPS) as i:
                act.wait_ge(ctxT_ps, at(i, 1, 1))
                act.activation(ctxT[:, :], ps[:, 6, :], ACT.Copy).then_inc(ctxT_sb, 1)
                act.activation(ctx2[:, :, :, :],
                               spread(ps[:, 6, :].rearrange("p (b a t) -> p b a t", b=BPG, a=1), 2, 2),
                               ACT.Copy).then_inc(ctx2_sb, 1)
                act.wait_ge(kT_ps, at(i, 1, 1))
                act.activation(kT[:, :], ps[:, 4, :], ACT.Copy).then_inc(kT_sb, 1)
                act.wait_ge(xnT_ps, at(i, 4, 1))
                act.activation(xnT[:, :], ps[:, 7, :], ACT.Copy).then_inc(xnT_sb, 1)
                act.wait_ge(vx_clear, 4)
                act.wait_ge(v_ps, at(i, 1, 1))
                for m in range(2):
                    half = slice(SEQ * m, SEQ * m + SEQ)
                    act.activation(v_half(vxh, half, m), v_src(half, m), ACT.Copy).then_inc(v_hi, 1)
                act.wait_ge(qT_ps, at(i, 1, 1))
                for g in range(ROWG):
                    rows = slice(32 * g, 32 * g + 32)
                    act.activation(qm[rows, :, g % 2, g // 2, :],
                                   ps[rows, 5, :].rearrange("p (b t) -> p b t", b=BPG), ACT.Copy).then_inc(qT_sb, 1)
                act.wait_ge(k1_ps, at(i, 1, 1))
                act.activation(k1T[:, :], ps[:, 4, :], ACT.Copy).then_inc(k1_sb, 1)
                act.wait_ge(v1_ps, at(i, 1, 1))
                act.activation(v1[:, :, :], ps[:, 6, :], ACT.Copy).then_inc(v1_sb, 1)

                def exp0(t):
                    act.wait_ge(s_sub, at(i, TILES, t + 1))
                    if t >= 2:
                        act.wait_ge(pT_ps, at(i, TILES, t - 1))
                    act.activation(prob[:, t % 2, :], ssub[:, t % 2, :], ACT.Exp, scale=SCALE0).then_inc(p_sb, 1)

                def phi(t):
                    act.wait_ge(pT_ps, at(i, TILES, t + 1))
                    if t >= 2:
                        act.wait_ge(o_ps, at(i, TILES, t - 1))
                    act.activation(ph[:, t % 2, :, :], ps[:, 4:6, :].rearrange("p a (b c) -> p (a b) c", c=P),
                                   ACT.Copy).then_inc(p_hi, 1)

                def ot(t):
                    act.wait_ge(oT_ps, at(i, TILES, t + 1))
                    for g in range(2):
                        for b in range(2):
                            act.activation(oT[SEQ * g:SEQ * g + SEQ, t % 2, SEQ * b:SEQ * b + SEQ],
                                           ps[SEQ * b:SEQ * b + SEQ, 6 + t % 2, 384 + SEQ * g:384 + SEQ * g + SEQ],
                                           ACT.Copy).then_inc(oT_sb, 1)

                exp0(0)
                exp0(1)
                phi(0)
                exp0(2)
                phi(1)
                exp0(3)
                ot(0)
                phi(2)
                ot(1)
                phi(3)
                ot(2)
                ot(3)
                act.wait_ge(xnT_ps, at(i, 4, 2))
                act.activation(xh[:, :], ps[:, 0, :], ACT.Copy).then_inc(xh_sb, 1)
                act.wait_ge(ls_sb, at(i, 1, 1))
                act.activation(ge[:, :, :], ls[:, :, :], ACT.Exp).then_inc(ge_sb, 1)

                def gt(t):
                    act.wait_ge(gT_ps, at(i, TILES, t + 1))
                    if t >= 2:
                        act.wait_ge(y1_ps, at(i, TILES, t - 1))
                    act.activation(gT[:, t % 2, :, :], ps[:, 0, 0:2 * P], ACT.Copy).then_inc(gT_sb, 1)

                for t in range(TILES):
                    for e in range(EXPERTS):
                        n = t * EXPERTS + e
                        act.wait_ge(h_ps, at(i, TILES * EXPERTS, n + 1))
                        if n >= RING:
                            act.wait_ge(g_sb, at(i, TILES * EXPERTS, n + 1 - RING))
                        act.activation(sg[:, n % RING, :], ps[:, 2 + n % RING, HID:UP], ACT.Sigmoid).then_inc(sg_sb, 1)
                        if t and e == 5:
                            gt(t - 1)
                gt(TILES - 1)
                act.wait_ge(xnT_ps, at(i, 4, 3))
                act.activation(xnT[:, :], ps[:, 2, :], ACT.Copy).then_inc(xnT_sb, 1)
                act.wait_ge(q1_ps, at(i, 1, 1))
                act.activation(q1T[:, :], ps[:, 3, :], ACT.Copy).then_inc(q1_sb, 1)
                act.wait_ge(nb1_sb, at(i, 1, 1))
                for t in range(TILES):
                    act.activation(p1[:, t, :], sm1[:, t, :], ACT.Exp, scale=SCALE1, bias=nb1[:, t:t + 1],
                                   accum_out=den1[:, t:t + 1]).then_inc(p1_sb, 1)
                act.wait_ge(p1T_ps, at(i, 1, 1))
                act.activation(p1T[:, :, :], ps[:, 5, :], ACT.Copy).then_inc(p1T_sb, 1)
                act.wait_ge(xnT_ps, at(i, 4, 4))
                act.wait_ge(vx_clear, 4)
                act.activation(x4p[:, :, 1:SEQ + 1], ps[:, 7, :].rearrange("p (b t) -> p b t", b=BPG),
                               ACT.Copy).then_inc(xnT_sb, 1)
                act.wait_ge(kf_ps, at(i, 1, 1))
                act.activation(krelu[:, :], ps[:, 2, :], ACT.Relu).then_inc(kr_sb, 1)
                act.wait_ge(kr_sb, at(i, 1, 1))
                act.activation(kact[:, :], krelu[:, :], ACT.Square).then_inc(kact_sb, 1)
                act.wait_ge(r_ps, at(i, 1, 1))
                act.activation(th[:, :], ps[:, 3, :], ACT.Tanh, scale=0.5).then_inc(th_sb, 1)

        @block.vector
        def _(dve):
            dve.memset(vxh[:, :, :, :, :, :], 0.0).then_inc(vx_clear, 1)
            dve.memset(vxl[:, :, :, :, :, :], 0.0).then_inc(vx_clear, 1)
            dve.memset(qm[:, :, :, :, :], 0.0).then_inc(vx_clear, 1)
            dve.memset(x4p[:, :, 0:1], 0.0).then_inc(vx_clear, 1)
            dve.memset(xout[:, 0:1, 0:1], 0.0).then_inc(xout_free, 16)
            dve.wait_ge(vx_clear, 1)
            for m in range(2):
                dve.memset(vxh[SEQ * m:SEQ * m + SEQ, :, :, :, m, HD:HD + 1], 1.0).then_inc(vx_ones, 1)
            dve.wait_ge(ld_mu, 32)
            dve.tensor_scalar(omu[:, :], mu[:, :], -1.0, 1.0, ALU.mult, ALU.add).then_inc(omu_s, 1)
            dve.wait_ge(ld_wg, 16)
            dve.tensor_scalar(wg_nat[:, 0:D - 1], wg_nat[:, 0:D - 1], wg_nat[:, D - 1:D], None,
                              ALU.subtract).then_inc(wg_adj, 1)
            dve.wait_ge(wg_adj, 1)
            dve.memset(wg_nat[:, D - 1:D], 0.0).then_inc(wg_adj, 1)
            dve.wait_ge(ld_w1, 16)
            for c in range(4):
                rows = slice(c * W1CH // 4, (c + 1) * W1CH // 4)
                dve.tensor_tensor(w1_nat[:, rows, 0:D - 1], w1_nat[:, rows, 0:D - 1],
                                  spread(w1_nat[:, rows, D - 1:D], 2, D - 1), ALU.subtract).then_inc(w1_sub, 1)
            dve.wait_ge(w1_sub, 4)
            dve.wait_ge(b1_ps, 1)
            dve.tensor_copy(w1_nat[:, :, D - 1], ps[:, 3, 0:W1CH]).then_inc(w1_adj, 1)
            dve.wait_ge(omu_s, 1)
            dve.wait_ge(wt_sb, 2)
            for r in range(2):
                dve.tensor_scalar(wmix[:, r, 0, :], wT[:, WR + r, :], omu[:, r:r + 1], None, ALU.mult)
                dve.tensor_scalar(wmix[:, r, 1, :], wT[:, WR + r, :], mu[:, r:r + 1], None,
                                  ALU.mult).then_inc(wmix_s, 1)
            dve.wait_ge(wt_sb, 3)
            dve.tensor_tensor(wgl[:, :], ps[:, 2, 2 * P:2 * P + EXPERTS], wgh[:, :], ALU.subtract).then_inc(wgl_s, 1)
            for e in range(EXPERTS):
                dve.wait_ge(w1_hi, e + 1)
                dve.tensor_tensor(w1l[:, e, :], ps[:, 4 + e % 4, :], w1h[:, e, :], ALU.subtract).then_inc(w1_lo, 1)

            with dve.Fori(0, GROUPS) as i:
                count = [0]

                def settle(ins, apart=False):
                    count[0] += 1
                    ins.then_inc(st, 1)
                    dve.wait_ge(st, at(i, SETTLES, count[0]))
                    if apart:
                        dve.memset(spare[:, :], 0.0)

                def layer_norm(n, src, last=False):
                    for t in range(TILES):
                        done = dve.bn_stats(stats[:, t, :], src[:, t, :])
                    settle(done, apart=True)
                    for t in range(TILES):
                        done = dve.bn_aggr(mv[:, t, :], stats[:, t, :])
                    done.then_inc(ln_var, 1)
                    w = D - 1 if last else D
                    if last:
                        dve.memset(xn[:, :, D - 1:D], 1.0)
                    dve.wait_ge(ln_rstd, at(i, 4, n))
                    for t in range(TILES):
                        dve.tensor_scalar(xn[:, t, 0:w], src[:, t, 0:w], mv[:, t, 0:1], rstd[:, t:t + 1],
                                          ALU.subtract, ALU.mult).then_inc(xn_sb, 1)

                dve.wait_ge(xin_in, at(i, 16, 16))
                layer_norm(1, xin)
                for m in range(2):
                    half = slice(SEQ * m, SEQ * m + SEQ)
                    dve.wait_ge(v_hi, at(i, 2, 2))
                    dve.tensor_tensor(v_half(vxl, half, m), v_src(half, m), v_half(vxh, half, m),
                                      ALU.subtract).then_inc(v_lo, 1)

                def smax(t):
                    s2 = ps[:, 2 * (t % 2):2 * (t % 2) + 2, :].rearrange("p a (h c) -> p (a h) c", c=SEQ)
                    dve.wait_ge(s_ps, at(i, TILES, t + 1))
                    settle(dve.tensor_reduce(mx[:, t % 2, :], s2, AX.X, ALU.max))
                    if t >= 2:
                        dve.wait_ge(p_sb, at(i, TILES, t - 1))
                    dve.tensor_tensor(ssub[:, t % 2, :].rearrange("p (h c) -> p h c", c=SEQ), s2,
                                      spread(mx[:, t % 2, :].unsqueeze(2), 2, SEQ), ALU.subtract).then_inc(s_sub, 1)

                def plo(t):
                    dve.wait_ge(p_hi, at(i, TILES, t + 1))
                    dve.tensor_tensor(pl[:, t % 2, :, :], ps[:, 4:6, :].rearrange("p a (b c) -> p (a b) c", c=P),
                                      ph[:, t % 2, :, :], ALU.subtract).then_inc(p_lo, 1)

                def norm(t):
                    dve.wait_ge(o_ps, at(i, TILES, t + 1))
                    o = ps[:, 6 + t % 2, 0:288].rearrange("p (b g h w) -> p b g h w", b=2, g=2, w=HD + 1)
                    for g in range(2):
                        half = slice(SEQ * g, SEQ * g + SEQ)
                        done = dve.reciprocal(rden[half, :].rearrange("p (b h) -> p b h", b=2), o[half, :, g, :, HD])
                    settle(done)
                    for g in range(2):
                        half = slice(SEQ * g, SEQ * g + SEQ)
                        for b in range(2):
                            dve.tensor_tensor(
                                onorm[half, t % 2, SEQ * b:SEQ * b + SEQ].rearrange("p (h d) -> p h d", d=HD),
                                o[half, b, g, :, 0:HD],
                                spread(rden[half, 8 * b:8 * b + 8].unsqueeze(2), 2, HD), ALU.mult).then_inc(o_nrm, 1)

                def x1(t):
                    dve.wait_ge(xb_sb, at(i, 1, 1))
                    dve.wait_ge(y0_ps, at(i, TILES, t + 1))
                    done = dve.tensor_tensor(xres[:, t, :], ps[:, 6 + t % 2, 0:P], xres[:, t, :], ALU.add)
                    settle(done) if t == TILES - 1 else done.then_inc(x1_sb, 1)

                smax(0)
                smax(1)
                plo(0)
                smax(2)
                norm(0)
                plo(1)
                smax(3)
                x1(0)
                norm(1)
                plo(2)
                x1(1)
                norm(2)
                plo(3)
                x1(2)
                norm(3)
                x1(3)

                layer_norm(2, xres, last=True)
                dve.wait_ge(xh_sb, at(i, 1, 1))
                dve.tensor_tensor(xl[:, :], ps[:, 0, :], xh[:, :], ALU.subtract).then_inc(xl_sb, 1)

                dve.wait_ge(lg_ps, at(i, 1, 1))
                settle(dve.tensor_copy(lg[:, :, :], ps[:, 1, 0:TILES * EXPERTS]), apart=True)
                for t in range(TILES):
                    done = dve.max(top[:, t, :], lg[:, t, :])
                settle(done)
                dve.tensor_tensor(ls[:, :, :], lg[:, :, :], spread(top[:, :, 0:1], 2, EXPERTS),
                                  ALU.subtract).then_inc(ls_sb, 1)
                for t in range(TILES):
                    done = dve.max_index(topi[:, t, :], top[:, t, :], lg[:, t, :])
                settle(done)
                settle(dve.tensor_copy(topf[:, :, :], topi[:, :, 0:2]))
                ie = spread(iota_e[:, :].unsqueeze(1), 1, TILES)
                dve.wait_ge(c_iota, 2)
                dve.tensor_tensor(sel0[:, :, :], ie, spread(topf[:, :, 0:1], 2, EXPERTS), ALU.is_equal)
                settle(dve.tensor_tensor(sel1[:, :, :], ie, spread(topf[:, :, 1:2], 2, EXPERTS), ALU.is_equal))
                settle(dve.tensor_tensor(sel0[:, :, :], sel0[:, :, :], sel1[:, :, :], ALU.add))
                dve.wait_ge(ge_sb, at(i, 1, 1))
                dve.tensor_reduce(zsum[:, :], ge[:, :, :], AX.X, ALU.add)
                settle(dve.tensor_tensor(es[:, :, :], ge[:, :, :], sel0[:, :, :], ALU.mult))
                settle(dve.tensor_reduce(ssum[:, :], es[:, :, :], AX.X, ALU.add))
                settle(dve.scalar_tensor_tensor(gden[:, :], zsum[:, :], EPS_GATE, ssum[:, :], ALU.mult, ALU.add))
                settle(dve.reciprocal(gden[:, :], gden[:, :]))
                dve.tensor_tensor(csum[:, :], ssum[:, :], gden[:, :], ALU.mult)
                settle(dve.tensor_tensor(comb[:, :, :], es[:, :, :], spread(gden[:, :].unsqueeze(2), 2, EXPERTS),
                                         ALU.mult))
                dve.wait_ge(ld_bof, 16)
                for t in range(TILES):
                    done = dve.scalar_tensor_tensor(xres[:, t, :], bof[:, :], csum[:, t:t + 1], xres[:, t, :],
                                                    ALU.mult, ALU.add)
                settle(done)

                def add_up(t):
                    dve.wait_ge(acc_pool, at(i, TILES * (POOL_E - 1), (t + 1) * (POOL_E - 1)))
                    dve.tensor_tensor(accd[:, t % 2, :], accd[:, t % 2, :], accp[:, t % 2, :],
                                      ALU.add).then_inc(acc_sb, 1)

                def x2(t):
                    dve.wait_ge(y1_ps, at(i, TILES, t + 1))
                    done = dve.tensor_tensor(xres[:, t, :], ps[:, 1, 0:P], xres[:, t, :], ALU.add)
                    done.then_inc(x2_sb, 1)

                for t in range(TILES):
                    for e in range(EXPERTS):
                        n = t * EXPERTS + e
                        dve.wait_ge(sg_sb, at(i, TILES * EXPERTS, n + 1))
                        if e < POOL_E:
                            m = t * POOL_E + e
                            g_out = gb[:, m % GBUF, :]
                            if m >= GBUF:
                                mt, me = divmod(m - GBUF, POOL_E)
                                dve.wait_ge(acc_pool, at(i, TILES * (POOL_E - 1), mt * (POOL_E - 1) + max(me, 1)))
                        else:
                            g_out = g67[:, e - POOL_E, :]
                        done = dve.scalar_tensor_tensor(g_out, ps[:, 2 + n % RING, 0:HID], comb[:, t, e:e + 1],
                                                        sg[:, n % RING, :], ALU.mult, ALU.mult)
                        done.then_inc(g_sb, 1)
                        if e == EXPERTS - 1:
                            dve.wait_ge(g_sb, at(i, TILES * EXPERTS, n + 1))
                            if t >= 2:
                                dve.wait_ge(gT_ps, at(i, TILES, t - 1))
                            settle(dve.tensor_tensor(accd[:, t % 2, :], g67[:, 0, :], g67[:, 1, :], ALU.add))
                        if t and e == 2:
                            add_up(t - 1)
                        if t and e == 6:
                            x2(t - 1)
                add_up(TILES - 1)
                x2(TILES - 1)
                dve.wait_ge(x2_sb, at(i, TILES, TILES))
                layer_norm(3, xres)

                dve.wait_ge(s1_ps, at(i, 1, 1))
                dve.wait_ge(c_cau, 3)
                settle(dve.tensor_tensor(sm1[:, :, :], ps[:, 4, :].rearrange("p (n c) -> p n c", c=P),
                                         spread(causal[:, :].unsqueeze(1), 1, TILES), ALU.add))
                settle(dve.tensor_reduce(mx1[:, :], sm1[:, :, :], AX.X, ALU.max))
                dve.tensor_scalar(nb1[:, :], mx1[:, :], -SCALE1, None, ALU.mult).then_inc(nb1_sb, 1)
                dve.wait_ge(p1_sb, at(i, TILES, TILES))
                settle(dve.reciprocal(rd1[:, :], den1[:, :]))
                dve.wait_ge(y2_ps, at(i, 1, 1))
                for t in range(TILES):
                    done = dve.scalar_tensor_tensor(xres[:, t, :], ps[:, 6, bass.ts(t, P)], rd1[:, t:t + 1],
                                                    xres[:, t, :], ALU.mult, ALU.add)
                settle(done)
                layer_norm(4, xres)
                dve.wait_ge(th_sb, at(i, 1, 1))
                dve.wait_ge(vf_ps, at(i, 1, 1))
                done = dve.scalar_tensor_tensor(uu[:, :], th[:, :], 1.0, ps[:, 4, :], ALU.add, ALU.mult)
                done.then_inc(u_sb, 1)
                dve.wait_ge(uT_ps, at(i, 1, 1))
                dve.wait_ge(xout_free, at(i, 16, 16))
                dve.scalar_tensor_tensor(xout[:, :, :], ps[:, 5, :].rearrange("p (n d) -> p n d", d=D), 0.5,
                                         xres[:, :, :], ALU.mult, ALU.add).then_inc(xo_sb, 1)
                assert count[0] == SETTLES, count

        @block.tensor
        def _(pe):
            pe.wait_ge(c_ident, 1)
            pe.wait_ge(ld_sq, 16 * SQ)
            for n in range(SQ):
                done = pe.transpose(ps[:, n // 4, bass.ts(n % 4, P)], w_nat[:, n, :], ident[:, :])
                if n % 4 == 3:
                    done.then_inc(wt_ps, 1)
            pe.wait_ge(ld_small, 32)
            pe.wait_ge(wg_adj, 2)
            for j in range(2):
                pe.transpose(ps[:, 2, bass.ts(j, P)], wof_nat[:, j, :], ident[:, :])
            pe.transpose(ps[:, 2, 2 * P:2 * P + EXPERTS], wg_nat[:, :], ident[0:EXPERTS, 0:EXPERTS]).then_inc(wt_ps, 1)
            pe.transpose(ps[:, 3, 0:W1CH], b1_nat[:, :], ident[0:W1CH, 0:W1CH]).then_inc(b1_ps, 1)
            pe.wait_ge(w1_adj, 1)
            for e in range(EXPERTS):
                if e >= 4:
                    pe.wait_ge(w1_lo, e - 3)
                for j in range(4):
                    done = pe.transpose(ps[:, 4 + e % 4, bass.ts(j, P)], w1_nat[:, 4 * e + j, :], ident[:, :])
                done.then_inc(w1_ps, 1)
            pe.wait_ge(wt_sb, 3)
            pe.wait_ge(wgl_s, 1)
            pe.wait_ge(w1_lo, EXPERTS)
            pe.wait_ge(wmix_s, 2)
            pe.wait_ge(vx_ones, 2)

            with pe.Fori(0, GROUPS) as i:
                def turn(n, bank):
                    for t in range(TILES):
                        pe.wait_ge(xn_sb, at(i, 4 * TILES, (n - 1) * TILES + t + 1))
                        done = pe.transpose(ps[:, bank, bass.ts(t, P)], xn[:, t, :], ident[:, :])
                    done.then_inc(xnT_ps, 1)

                pe.wait_ge(ln_var, at(i, 4, 1))
                pe.wait_ge(cin_in, at(i, 16, 16))
                for t in range(TILES):
                    done = pe.transpose(ps[:, 6, bass.ts(t, P)], cin[:, t, :], ident[:, :])
                done.then_inc(ctxT_ps, 1)
                pe.wait_ge(ctxT_sb, at(i, 1, 1))
                pe.matmul(ps[:, 4, :], wT[:, WK0, :], ctxT[:, :], start=True, stop=True).then_inc(kT_ps, 1)
                turn(1, 7)
                pe.wait_ge(ctx2_sb, at(i, 1, 1))
                for b in range(BPG):
                    done = pe.matmul(ps[:, 2 + b // 4, bass.ts(b % 4, P)], ctx2[:, b, :, :],
                                     wT[:, WV0, :], start=True, stop=True)
                done.then_inc(v_ps, 1)
                pe.wait_ge(xnT_sb, at(i, 3, 1))
                pe.matmul(ps[:, 5, :], wT[:, WQ0, :], xnT[:, :], start=True, stop=True).then_inc(qT_ps, 1)
                pe.wait_ge(kT_sb, at(i, 1, 1))
                pe.matmul(ps[:, 4, :], wT[:, WQ1, :], ctxT[:, :], start=True, stop=True).then_inc(k1_ps, 1)
                for t in range(TILES):
                    done = pe.matmul(ps[:, 6, bass.ts(t, P)], ctxT[:, bass.ts(t, P)], wT[:, WQ1, :],
                                     start=True, stop=True)
                done.then_inc(v1_ps, 1)

                def scores(t):
                    pe.wait_ge(qT_sb, at(i, ROWG, ROWG))
                    pe.wait_ge(kbd_sb, at(i, BPG, 2 * t + 2))
                    if t == 1:
                        pe.wait_ge(v_lo, at(i, 2, 2))
                    if t >= 2:
                        pe.wait_ge(s_sub, at(i, TILES, t - 1))
                    for b in range(2):
                        for g in range(2):
                            done = pe.matmul(ps[:, 2 * (t % 2) + b, 256 * g:256 * g + 256],
                                             qm[:, 2 * t + b, g, :, :], kbd[:, 2 * t + b, :, :],
                                             start=True, stop=True)
                    done.then_inc(s_ps, 1)

                def turn_p(t):
                    pe.wait_ge(p_sb, at(i, TILES, t + 1))
                    if t == 0:
                        pe.wait_ge(k1_sb, at(i, 1, 1))
                    else:
                        pe.wait_ge(p_lo, at(i, TILES, t))
                    for c in range(PAIRS):
                        done = pe.transpose(ps[:, 4 + c // 4, bass.ts(c % 4, P)], prob[:, t % 2, bass.ts(c, P)],
                                            ident[:, :])
                    done.then_inc(pT_ps, 1)

                def pv(t):
                    pe.wait_ge(p_lo, at(i, TILES, t + 1))
                    if t == 0:
                        pe.wait_ge(v1_sb, at(i, 1, 1))
                    if t >= 2:
                        pe.wait_ge(x1_sb, at(i, TILES - 1, t - 1))
                    for b in range(2):
                        for c in range(4):
                            o = ps[:, 6 + t % 2, 0:288].rearrange("p (b g h w) -> p b g h w", b=2, g=2, h=4)[:, b, :, c, :]
                            vh = vxh[:, 2 * t + b, :, c, :, :].rearrange("p g m w -> p g (m w)")
                            vl = vxl[:, 2 * t + b, :, c, :, :].rearrange("p g m w -> p g (m w)")
                            pe.matmul(o, ph[:, t % 2, 4 * b + c, :], vh, start=True, stop=False)
                            pe.matmul(o, ph[:, t % 2, 4 * b + c, :], vl, start=False, stop=False)
                            done = pe.matmul(o, pl[:, t % 2, 4 * b + c, :], vh, start=False, stop=True)
                    done.then_inc(o_ps, 1)

                def turn_o(t):
                    pe.wait_ge(o_nrm, at(i, 4 * TILES, 4 * t + 4))
                    pe.transpose(ps[:, 6 + t % 2, 384:512], onorm[:, t % 2, :], ident[:, :]).then_inc(oT_ps, 1)

                def out0(t):
                    pe.wait_ge(oT_sb, at(i, 4 * TILES, 4 * t + 4))
                    pe.matmul(ps[:, 6 + t % 2, 0:P], oT[:, t % 2, :], wT[:, WO0, :],
                              start=True, stop=True).then_inc(y0_ps, 1)

                scores(0)
                scores(1)
                turn_p(0)
                scores(2)
                pv(0)
                turn_p(1)
                scores(3)
                turn_o(0)
                pv(1)
                out0(0)
                turn_p(2)
                turn_o(1)
                out0(1)
                pv(2)
                turn_p(3)
                turn_o(2)
                out0(2)
                pv(3)
                turn_o(3)
                out0(3)

                turn(2, 0)
                pe.wait_ge(xh_sb, at(i, 1, 1))
                pe.wait_ge(xl_sb, at(i, 1, 1))
                for t in range(TILES):
                    o = ps[:, 1, EXPERTS * t:EXPERTS * t + EXPERTS]
                    pe.matmul(o, xh[:, bass.ts(t, P)], wgh[:, :], start=True, stop=False)
                    pe.matmul(o, xh[:, bass.ts(t, P)], wgl[:, :], start=False, stop=False)
                    done = pe.matmul(o, xl[:, bass.ts(t, P)], wgh[:, :], start=False, stop=True)
                done.then_inc(lg_ps, 1)

                def turn_g(t):
                    pe.wait_ge(acc_sb, at(i, TILES, t + 1))
                    if t >= 1:
                        pe.wait_ge(gT_sb, at(i, TILES, t))
                    for j in range(2):
                        done = pe.transpose(ps[:, 0, bass.ts(j, P)], accd[:, t % 2, bass.ts(j, P)], ident[:, :])
                    done.then_inc(gT_ps, 1)

                def out1(t):
                    pe.wait_ge(gT_sb, at(i, TILES, t + 1))
                    if t >= 1:
                        pe.wait_ge(x2_sb, at(i, TILES, t))
                    for j in range(2):
                        done = pe.matmul(ps[:, 1, 0:P], gT[:, t % 2, j, :], wofT[:, j, :],
                                         start=(j == 0), stop=(j == 1))
                    done.then_inc(y1_ps, 1)

                for t in range(TILES):
                    for e in range(EXPERTS):
                        n = t * EXPERTS + e
                        o = ps[:, 2 + n % RING, :]
                        if n >= RING:
                            pe.wait_ge(g_sb, at(i, TILES * EXPERTS, n + 1 - RING))
                        pe.matmul(o, xh[:, bass.ts(t, P)], w1h[:, e, :], start=True, stop=False)
                        pe.matmul(o, xh[:, bass.ts(t, P)], w1l[:, e, :], start=False, stop=False)
                        pe.matmul(o, xl[:, bass.ts(t, P)], w1h[:, e, :], start=False, stop=True).then_inc(h_ps, 1)
                        if t and e == 4:
                            turn_g(t - 1)
                        if t and e == 6:
                            out1(t - 1)
                turn_g(TILES - 1)
                out1(TILES - 1)

                turn(3, 2)
                pe.wait_ge(xnT_sb, at(i, 3, 2))
                pe.matmul(ps[:, 3, :], wT[:, WQ1, :], xnT[:, :], start=True, stop=True).then_inc(q1_ps, 1)
                pe.wait_ge(q1_sb, at(i, 1, 1))
                for t in range(TILES):
                    done = pe.matmul(ps[:, 4, bass.ts(t, P)], q1T[:, bass.ts(t, P)], k1T[:, bass.ts(t, P)],
                                     start=True, stop=True)
                done.then_inc(s1_ps, 1)
                for t in range(TILES):
                    pe.wait_ge(p1_sb, at(i, TILES, t + 1))
                    done = pe.transpose(ps[:, 5, bass.ts(t, P)], p1[:, t, :], ident[:, :])
                done.then_inc(p1T_ps, 1)
                pe.wait_ge(p1T_sb, at(i, 1, 1))
                for t in range(TILES):
                    done = pe.matmul(ps[:, 6, bass.ts(t, P)], p1T[:, t, :], v1[:, t, :], start=True, stop=True)
                done.then_inc(y2_ps, 1)
                turn(4, 7)
                pe.wait_ge(xnT_sb, at(i, 3, 3))
                pe.matmul(ps[:, 2, :], wmix[:, 1, 0, :], x4p[:, :, 0:SEQ], start=True, stop=False)
                pe.matmul(ps[:, 2, :], wmix[:, 1, 1, :], x4p[:, :, 1:SEQ + 1], start=False, stop=True).then_inc(kf_ps, 1)
                pe.matmul(ps[:, 3, :], wmix[:, 0, 0, :], x4p[:, :, 0:SEQ], start=True, stop=False)
                pe.matmul(ps[:, 3, :], wmix[:, 0, 1, :], x4p[:, :, 1:SEQ + 1], start=False, stop=True).then_inc(r_ps, 1)
                pe.wait_ge(kact_sb, at(i, 1, 1))
                pe.matmul(ps[:, 4, :], wT[:, WVF, :], kact[:, :], start=True, stop=True).then_inc(vf_ps, 1)
                pe.wait_ge(u_sb, at(i, 1, 1))
                for t in range(TILES):
                    done = pe.transpose(ps[:, 5, bass.ts(t, P)], uu[:, bass.ts(t, P)], ident[:, :])
                done.then_inc(uT_ps, 1)
    return nc


_INS = ['x', 'ctx_1024', 'L0_xattn_Wq', 'L0_xattn_Wk', 'L0_xattn_Wv', 'L0_xattn_Wo', 'L0_xattn_bo', 'L0_ffn_Wg',
        'L0_ffn_W1', 'L0_ffn_b1', 'L0_ffn_Wo', 'L0_ffn_bo', 'L1_xattn_Wq', 'L1_ffn_W_r', 'L1_ffn_W_k', 'L1_ffn_W_v',
        'L1_ffn_mu_r', 'L1_ffn_mu_k']


def kernel(**inputs):
    import numpy as _np
    import concourse.bacc as _bacc
    from concourse.bass_utils import run_bass_kernel_spmd as _run

    nc = _bacc.Bacc("TRN2", target_bir_lowering=False, num_devices=1)
    arrays, args = {}, []
    for name in _INS:
        a = _np.ascontiguousarray(inputs[name])
        arrays[f"in_{name}"] = a
        args.append(nc.dram_tensor(f"in_{name}", a.shape, mybir.dt.from_np(a.dtype), kind="ExternalInput").ap())
    args.append(nc.dram_tensor("out_x", (BATCH, SEQ, D), F32, kind="ExternalOutput").ap())
    build(nc, *args)
    r = _run(nc, [arrays], core_ids=[0])
    return r.results[0]["out_x"]
```

```python
import concourse.bass as bass
from concourse import mybir
from contextlib import ExitStack

F32 = mybir.dt.float32
F16 = mybir.dt.float16
U32 = mybir.dt.uint32
ALU = mybir.AluOpType
ACT = mybir.ActivationFunctionType
AX = mybir.AxisListType

P = 128
BATCH, SEQ, D = 32, 64, 128
HEADS = 16
HD = D // HEADS
PAIRS = HEADS // 2
ROWG = 4
HPG = HEADS // ROWG
EXPERTS, HID = 8, 256
UP = 2 * HID
TILES = 2
BPG = 2 * TILES
TOK = TILES * P
GROUPS = BATCH * SEQ // TOK
UNITS = BPG
GATES = 4
GBUF = 4
POOL_E = 6
EPS_LN = 1e-5
EPS_GATE = 1e-9
SCALE0 = float(D) ** -0.5
SCALE1 = float(D) ** -0.5
NEG = -1e30

SC, PT, AO, HB, L1, F0 = 0, 2, 3, 4, 6, 7

PE_ORDER = """V1+1 E7+1 E8+1 T2+1 C_p+1 O0+1 E9+1 C_y+1 F_T+1 Y0+1 E10+1 E11+1 T3+1 F_q+1 E12+1 C_x4+1 V2+1 E13+1 V3+1 S0 G0+1
S1 O1+1 E14+1 H0+1 E15+1 Y1+1 F_v+1 C_kr+1 S2 G1+1 B_T C_v+1 H1+1 B_gate E0 T0 F_ctx E1 C_u+1 S3 F_k E2 E3 C_ctx
T1 C_T V0 E4 C_q E5 E6 C_s""".split()
ACT_ORDER = """E4+1 C_q+1 E5+1 E6+1 C_s+1 S2+1 E7+1 C_p+1 E8+1 O0+1 E9+1 T2+1 S3+1 F_T+1 E10+1 E11+1 T3+1 F_q+1 E12+1 C_x4+1
G0+1 E13+1 O1+1 E14+1 E15+1 S0 F_v+1 C_kr+1 G1+1 B_T S1 B_gate T0 F_ctx E0 E1 F_k E2 C_out+1 E3 C_T T1""".split()
DVE_ORDER = """T0+1 C_T+1 E2+1 E3+1 S2+1 E4+1 T1+1 E5+1 F_T+1 E6+1 C_s+1 O0+1 E7+1 S3+1 C_y+1 E8+1 E9+1 C_ln4+1 T2+1 F_ln E10+1
Y0+1 C_x4+1 E11+1 T3+1 G0+1 O1+1 E12+1 S0 E13+1 S1 H0+1 E14+1 Y1+1 E15+1 B_ln G1+1 F_v+1 B_T C_v+1 H1+1 B_gate
E0 C_ln E1 C_u+1""".split()
POOL_ORDER = """K2+1 E4+1 C_ln4+1 E5+1 E9+1 E10+1 F_ln K3+1 E11+1 E12+1 E13+1 B_ln C_ln E1 A_x E2 E3 K0 K1""".split()
SP_ORDER = """A_x F_ctx C_ln""".split()
PHASES = "FABC"
LAG = 1
LOOP_FROM = len(PHASES) + LAG
PHASE = {"S": "A", "T": "A", "V": "A", "O": "A", "Y": "A", "E": "B", "G": "B", "H": "B", "K": "F"}
SETTLES = {"F": 1, "A": 6, "B": 14, "C": 6}


def spread(ap, axis, n):
    shape = list(ap.shape)
    assert shape[axis] == 1
    shape[axis] = n
    return ap.broadcast_to(shape)


def build(nc, x, ctx_1024, L0_xattn_Wq, L0_xattn_Wk, L0_xattn_Wv, L0_xattn_Wo, L0_xattn_bo,
          L0_ffn_Wg, L0_ffn_W1, L0_ffn_b1, L0_ffn_Wo, L0_ffn_bo, L1_xattn_Wq,
          L1_ffn_W_r, L1_ffn_W_k, L1_ffn_W_v, L1_ffn_mu_r, L1_ffn_mu_k, out):
    x_dram = x.rearrange("b s d -> (b s) d").rearrange("(n p) d -> p n d", p=P)
    ctx_dram = ctx_1024.rearrange("b s d -> (b s) d").rearrange("(n p) d -> p n d", p=P)
    out_dram = out.rearrange("b s d -> (b s) d").rearrange("(n p) d -> p n d", p=P)

    with ExitStack() as stack:
        def sb(name, shape, dt=F32):
            return stack.enter_context(nc.sbuf_tensor(name, shape, dt))

        def sem(name):
            return stack.enter_context(nc.semaphore(name))

        SQ = 8
        WQ0, WK0, WV0, WO0, WQ1, WR, WKF, WVF = range(SQ)
        w_nat = sb("w_nat", [P, SQ, D])
        w1_nat = sb("w1_nat", [P, EXPERTS * UP // P, D])
        wof_nat = sb("wof_nat", [P, 2, P])
        wg_nat = sb("wg_nat", [EXPERTS, D])
        b1_nat = sb("b1_nat", [EXPERTS * UP // P, P])
        bo0 = sb("bo0", [P, D])
        bof = sb("bof", [P, D])
        mu = sb("mu", [P, 2])
        wT = sb("wT", [P, SQ, D])
        wmix = sb("wmix", [P, 2, 2, D])
        omu = sb("omu", [P, 2])
        w1h = sb("w1h", [P, EXPERTS, UP], F16)
        w1l = sb("w1l", [P, EXPERTS, UP], F16)
        wofT = sb("wofT", [P, 2, D])
        wgh = sb("wgh", [P, EXPERTS], F16)
        wgl = sb("wgl", [P, EXPERTS], F16)
        ident = sb("ident", [P, P])
        headmask = sb("headmask", [P, HPG, SEQ])
        causal = sb("causal", [P, P])
        hm0 = sb("hm0", [P, 3, HPG])
        hm1 = sb("hm1", [P, ROWG, HPG])
        iota_e = sb("iota_e", [P, EXPERTS])
        iota_i = sb("iota_i", [P, EXPERTS], mybir.dt.int32)
        eps_t = sb("eps_t", [P, TILES])
        mhalf = sb("mhalf", [P, TILES])
        spare = sb("spare", [P, 1])
        LN = "FBCD"
        stats = {n: sb("stats" + n, [P, TILES, 6]) for n in LN}
        mv = {n: sb("mv" + n, [P, TILES, 2]) for n in LN}
        vare = {n: sb("vare" + n, [P, TILES]) for n in LN}
        rstd = {n: sb("rstd" + n, [P, TILES]) for n in LN}
        xn = {n: sb("xn" + n, [P, TILES, D]) for n in LN}
        xin = sb("xin", [P, TILES, D])
        cin = sb("cin", [P, TILES, D])
        ctxT = sb("ctxT", [P, TOK])
        ctx2 = sb("ctx2", [P, BPG, 2, SEQ])
        kT = sb("kT", [P, TOK])
        xnT = sb("xnT", [P, TOK])
        qm = sb("qm", [P, BPG, 2, 2, SEQ])
        kbd = sb("kbd", [P, BPG, HPG, SEQ])
        vxh = sb("vxh", [P, BPG, 2, 4, 2, HD + 1], F16)
        vxl = sb("vxl", [P, BPG, 2, 4, 2, HD + 1], F16)
        xa = sb("xa", [P, TILES, D])
        xb = sb("xb", [P, TILES, D])
        HS = HEADS * SEQ // 2
        mx = sb("mx", [P, 2, HS // SEQ])
        ssub = sb("ssub", [P, 2, HS])
        prob = sb("prob", [P, 2, HS])
        ph = sb("ph", [P, 2, 4, P], F16)
        pl = sb("pl", [P, 2, 4, P], F16)
        rden = sb("rden", [P, 2, HEADS // 2])
        onorm = sb("onorm", [P, 2, D])
        oT = sb("oT", [P, 2, P])
        x1 = sb("x1", [P, TILES, D])
        xh = sb("xh", [P, TOK], F16)
        xl = sb("xl", [P, TOK], F16)
        lg = sb("lg", [P, TILES, EXPERTS])
        top = sb("top", [P, TILES, 8])
        topi = sb("topi", [P, TILES, 8], U32)
        topf = sb("topf", [P, TILES, 2])
        ls = sb("ls", [P, TILES, EXPERTS])
        ge = sb("ge", [P, TILES, EXPERTS])
        sel0 = sb("sel0", [P, TILES, EXPERTS])
        sel1 = sb("sel1", [P, TILES, EXPERTS])
        es = sb("es", [P, TILES, EXPERTS])
        ssum = sb("ssum", [P, TILES])
        zsum = sb("zsum", [P, TILES])
        gden = sb("gden", [P, TILES])
        comb = sb("comb", [P, TILES, EXPERTS])
        csum = sb("csum", [P, TILES])
        xB = sb("xB", [P, TILES, D])
        th = sb("th", [P, GATES, HID])
        sg = sb("sg", [P, GATES, HID])
        gb = sb("gb", [P, GBUF, HID])
        accp = sb("accp", [P, 2, HID])
        accd = sb("accd", [P, 2, HID])
        g67 = sb("g67", [P, 2, HID])
        gT = sb("gT", [P, 2, 2, P])
        x2 = sb("x2", [P, TILES, D])
        cinc = sb("cinc", [P, TILES, D])
        cx = sb("cx", [P, 2 * TOK])
        kq = sb("kq", [P, 2 * TOK])
        v1 = sb("v1", [P, TILES, D])
        sm1 = sb("sm1", [P, TILES, P])
        mx1 = sb("mx1", [P, TILES])
        nb1 = sb("nb1", [P, TILES])
        den1 = sb("den1", [P, TILES])
        rd1 = sb("rd1", [P, TILES])
        p1 = sb("p1", [P, TILES, P])
        p1T = sb("p1T", [P, TILES, P])
        x3 = sb("x3", [P, TILES, D])
        x4p = sb("x4p", [P, BPG, SEQ + 1])
        krelu = sb("krelu", [P, TOK])
        kact = sb("kact", [P, TOK])
        thr = sb("thr", [P, TOK])
        uu = sb("uu", [P, TOK])
        xout = sb("xout", [P, TILES, D])

        ps = stack.enter_context(nc.psum_tensor("ps", [P, 8, 512], F32))

        ld_sq = sem("ld_sq")
        ld_bo0 = sem("ld_bo0")
        ld_bof = sem("ld_bof")
        ld_wg = sem("ld_wg")
        ld_mu = sem("ld_mu")
        ld_w1 = sem("ld_w1")
        ld_small = sem("ld_small")
        c_id0 = sem("c_id0")
        c_ident = sem("c_ident")
        c_pow = sem("c_pow")
        c_hm = sem("c_hm")
        c_cau = sem("c_cau")
        c_iota = sem("c_iota")
        cleared = sem("cleared")
        vx_ones = sem("vx_ones")
        wt_ps = sem("wt_ps")
        wt_sb = sem("wt_sb")
        omu_s = sem("omu_s")
        wmix_s = sem("wmix_s")
        wgl_s = sem("wgl_s")
        b1_ps = sem("b1_ps")
        w1_sub = sem("w1_sub")
        w1_adj = sem("w1_adj")
        wg_adj = sem("wg_adj")
        w1_ps = sem("w1_ps")
        w1_hi = sem("w1_hi")
        w1_lo = sem("w1_lo")
        settled = {n: sem("settled" + n) for n in SETTLES}
        ln_var = {n: sem("ln_var" + n) for n in LN}
        ln_ve = {n: sem("ln_ve" + n) for n in LN}
        ln_rstd = {n: sem("ln_rstd" + n) for n in LN}
        xn_sb = {n: sem("xn_sb" + n) for n in LN}
        xnT_ps = {n: sem("xnT_ps" + n) for n in LN}
        (xin_in, cin_in, xa_in, cinc_in, ctxT_ps, ctxT_sb, kT_ps, kT_sb, xnT_sb, qT_ps, qm_sb, kbd_sb, v_ps, v_hi,
         v_lo) = map(sem, ("xin_in cin_in xa_in cinc_in ctxT_ps ctxT_sb kT_ps kT_sb xnT_sb qT_ps qm_sb kbd_sb v_ps "
                           "v_hi v_lo").split())
        (xb_sb, s_ps, s_sub, p_sb, pT_ps, p_hi, p_lo, o_ps, o_nrm, oT_ps, oT_sb, y0_ps, x1_sb) = map(
            sem, "xb_sb s_ps s_sub p_sb pT_ps p_hi p_lo o_ps o_nrm oT_ps oT_sb y0_ps x1_sb".split())
        (xh_sb, xl_sb, lg_ps, lg_sb, ls_sb, ge_sb, comb_sb, h_ps, th_sb, sg_sb, g_sb, acc_pool, acc_sb, gT_ps, gT_sb,
         y1_ps, x2_sb) = map(sem, ("xh_sb xl_sb lg_ps lg_sb ls_sb ge_sb comb_sb h_ps th_sb sg_sb g_sb acc_pool "
                                   "acc_sb gT_ps gT_sb y1_ps x2_sb").split())
        (cc_ps, cx_sb, kq_ps, kq_sb, s1_ps, v1_sb, nb1_sb, p1_sb, p1T_ps, p1T_sb, y2_ps, x4_sb, kr_ps, krelu_sb,
         kact_sb, thr_sb, vf_ps, u_sb, uT_ps, xo_sb) = map(
            sem, ("cc_ps cx_sb kq_ps kq_sb s1_ps v1_sb nb1_sb p1_sb p1T_ps p1T_sb y2_ps x4_sb kr_ps krelu_sb "
                  "kact_sb thr_sb vf_ps u_sb uT_ps xo_sb").split())
        xout_free = sem("xout_free")

        W1B = (HB, HB + 1, L1)
        W1CH = EXPERTS * UP // P
        ADDS = TILES * (POOL_E - 1)
        EXP = TILES * EXPERTS
        block = stack.enter_context(nc.Block())

        def v_src(half, m):
            v = ps[half, F0, :].rearrange("p (b c) -> p b c", c=SEQ)
            return v.rearrange("p n (h m d) -> p n h m d", m=2, d=HD)[:, :, :, m, :]

        def v_half(buf, half, m):
            return buf[half, :, :, :, m, 0:HD].rearrange("p b g h d -> p (b g) h d")

        def at(i, per, k):
            return i * per + k

        def wait(eng, s, value):
            if not isinstance(value, int) or value > 0:
                eng.wait_ge(s, value)

        def steps(eng, order, stage, prepare=None):
            stages = []
            for entry in order:
                name, _, lag = entry.partition("+")
                phase = PHASE[name[0]] if name[1:].isdigit() else name[0]
                stages.append((name, PHASES.index(phase) + int(lag or 0)))

            def step(s, some):
                for name, behind in stages:
                    if some and not 0 <= s - behind < GROUPS:
                        continue
                    n = int(name[1:]) if name[1:].isdigit() else None
                    stage(name[0] if n is not None else name, n, s - behind if behind else s)

            for s in range(LOOP_FROM):
                step(s, True)
                if s == 0 and prepare:
                    prepare()
            with eng.Fori(LOOP_FROM, GROUPS) as s:
                step(s, False)
            for s in range(GROUPS, GROUPS + len(PHASES) - 1 + LAG):
                step(s, True)

        @block.sync
        def _(sp):
            squares = [L0_xattn_Wq, L0_xattn_Wk, L0_xattn_Wv, L0_xattn_Wo, L1_xattn_Wq,
                       L1_ffn_W_r, L1_ffn_W_k, L1_ffn_W_v]

            def stage(name, n, i):
                if name == "F_ctx":
                    wait(sp, ctxT_ps, at(i, 1, 0))
                    sp.dma_start(cin[:, :, :], ctx_dram[:, bass.ts(i, TILES), :]).then_inc(cin_in, 16)
                    wait(sp, xn_sb["F"], at(i, TILES, 0))
                    sp.dma_start(xin[:, :, :], x_dram[:, bass.ts(i, TILES), :]).then_inc(xin_in, 16)
                    if isinstance(i, int) and i == 0:
                        for n in range(SQ):
                            sp.dma_start(w_nat[:, n, :], squares[n]).then_inc(ld_sq, 16)
                        sp.dma_start(bo0[:, :], spread(L0_xattn_bo.rearrange("(a d) -> a d", a=1), 0, P)).then_inc(ld_bo0, 16)
                        sp.dma_start(w1_nat[:, :, :], L0_ffn_W1.rearrange("e (j p) d -> p (e j) d", p=P)).then_inc(ld_w1, 16)
                if name == "A_x":
                    wait(sp, xb_sb, at(i, 1, 0))
                    sp.dma_start(xa[:, :, :], x_dram[:, bass.ts(i, TILES), :]).then_inc(xa_in, 16)
                if name == "C_ln":
                    wait(sp, cc_ps, at(i, 1, 0))
                    sp.dma_start(cinc[:, :, :], ctx_dram[:, bass.ts(i, TILES), :]).then_inc(cinc_in, 16)

            steps(sp, SP_ORDER, stage)
            sp.wait_ge(xout_free, 16 * GROUPS + 16)

        @block.gpsimd
        def _(pool):
            pool.memset(ident[:, :], 0.0).then_inc(c_id0, 1)
            pool.wait_ge(c_id0, 1)
            pool.affine_select(out=ident[:, :], in_=ident[:, :], compare_op=ALU.not_equal, fill=1.0,
                               base=0, pattern=[[-1, P]], channel_multiplier=1).then_inc(c_ident, 1)
            pool.memset(eps_t[:, :], EPS_LN)
            pool.memset(mhalf[:, :], -0.5).then_inc(c_pow, 1)
            pool.memset(hm0[:, :, :], 0.0).then_inc(c_hm, 1)
            pool.wait_ge(c_hm, 1)
            pool.memset(hm1[:, :, :], 1.0).then_inc(c_hm, 1)
            pool.wait_ge(c_hm, 2)
            pool.affine_select(out=hm1[:, :, :], in_=hm1[:, :, :], compare_op=ALU.is_ge, fill=0.0,
                               base=0, pattern=[[-32, ROWG], [-HD, HPG]], channel_multiplier=1).then_inc(c_hm, 1)
            pool.wait_ge(c_hm, 3)
            pool.affine_select(out=hm1[:, :, :], in_=hm1[:, :, :], compare_op=ALU.is_ge, fill=0.0,
                               base=HD - 1, pattern=[[32, ROWG], [HD, HPG]], channel_multiplier=-1).then_inc(c_hm, 1)
            pool.wait_ge(c_hm, 4)
            pool.tensor_tensor(hm0[:, 0, :], hm1[:, 0, :], hm1[:, 1, :], ALU.add)
            pool.tensor_tensor(hm0[:, 1, :], hm1[:, 2, :], hm1[:, 3, :], ALU.add).then_inc(c_hm, 1)
            pool.wait_ge(c_hm, 5)
            pool.tensor_tensor(hm0[:, 2, :], hm0[:, 0, :], hm0[:, 1, :], ALU.add).then_inc(c_hm, 1)
            pool.wait_ge(c_hm, 6)
            pool.tensor_copy(headmask[:, :, :], spread(hm0[:, 2, :].unsqueeze(2), 2, SEQ)).then_inc(c_hm, 1)
            pool.wait_ge(c_hm, 7)
            pool.memset(causal[:, :], 0.0).then_inc(c_cau, 1)
            pool.wait_ge(c_cau, 1)
            pool.affine_select(out=causal[:, :], in_=causal[:, :], compare_op=ALU.is_ge, fill=NEG,
                               base=0, pattern=[[-1, P]], channel_multiplier=1).then_inc(c_cau, 1)
            pool.wait_ge(c_cau, 2)
            pool.memset(causal[SEQ:P, 0:SEQ], NEG).then_inc(c_cau, 1)
            pool.wait_ge(c_cau, 3)
            pool.iota(iota_i[:, :], [[1, EXPERTS]], base=0, channel_multiplier=0).then_inc(c_iota, 1)
            pool.wait_ge(c_iota, 1)
            pool.tensor_copy(iota_e[:, :], iota_i[:, :]).then_inc(c_iota, 1)

            def stage(name, n, i):
                ln = {"F_ln": "F", "B_ln": "B", "C_ln": "C", "C_ln4": "D"}.get(name)
                if ln:
                    pool.wait_ge(ln_var[ln], at(i, 1, 1))
                    pool.tensor_tensor(vare[ln][:, :], mv[ln][:, :, 1], eps_t[:, :], ALU.add).then_inc(ln_ve[ln], 1)
                    pool.wait_ge(ln_ve[ln], at(i, 1, 1))
                    pool.tensor_tensor(rstd[ln][:, :], vare[ln][:, :], mhalf[:, :], ALU.pow).then_inc(ln_rstd[ln], 1)
                if name == "A_x":
                    pool.wait_ge(xa_in, at(i, 16, 16))
                    pool.wait_ge(ld_bo0, 16)
                    wait(pool, x1_sb, at(i, TILES, 0))
                    pool.tensor_tensor(xb[:, :, :], xa[:, :, :], spread(bo0[:, :].unsqueeze(1), 1, TILES),
                                       ALU.add).then_inc(xb_sb, 1)
                if name == "K":
                    pool.wait_ge(kT_sb, at(i, 1, 1))
                    wait(pool, s_ps, at(i, UNITS, 0))
                    pool.tensor_tensor(kbd[:, n, :, :], spread(kT[:, bass.ts(n, SEQ)].unsqueeze(1), 1, HPG),
                                       headmask[:, :, :], ALU.mult).then_inc(kbd_sb, 1)
                if name == "E":
                    t, e = divmod(n, EXPERTS)
                    m = t * POOL_E + e
                    if 1 <= e < POOL_E:
                        pool.wait_ge(g_sb, at(i, EXP, n + 1))
                        if e == 1:
                            wait(pool, acc_sb, at(i, TILES, t - 1))
                            pool.tensor_tensor(accp[:, t % 2, :], gb[:, (m - 1) % GBUF, :], gb[:, m % GBUF, :],
                                               ALU.add).then_inc(acc_pool, 1)
                        else:
                            pool.wait_ge(acc_pool, at(i, ADDS, t * (POOL_E - 1) + e - 1))
                            pool.tensor_tensor(accp[:, t % 2, :], accp[:, t % 2, :], gb[:, m % GBUF, :],
                                               ALU.add).then_inc(acc_pool, 1)

            steps(pool, POOL_ORDER, stage)

        @block.scalar
        def _(act):
            act.dma_start(wof_nat[:, :, :], L0_ffn_Wo.rearrange("d (j p) -> d j p", p=P)).then_inc(ld_small, 16)
            act.dma_start(wg_nat[:, :], L0_ffn_Wg).then_inc(ld_wg, 16)
            act.dma_start(b1_nat[:, :], L0_ffn_b1.rearrange("e (j p) -> (e j) p", p=P)).then_inc(ld_small, 16)
            act.dma_start(bof[:, :], spread(L0_ffn_bo.rearrange("(a d) -> a d", a=1), 0, P)).then_inc(ld_bof, 16)
            act.dma_start(mu[:, 0:1], L1_ffn_mu_r.rearrange("(d a) -> d a", a=1)).then_inc(ld_mu, 16)
            act.dma_start(mu[:, 1:2], L1_ffn_mu_k.rearrange("(d a) -> d a", a=1)).then_inc(ld_mu, 16)
            for n in range(2):
                act.wait_ge(wt_ps, n + 1)
                act.activation(wT[:, 4 * n:4 * n + 4, :], ps[:, n, :], ACT.Copy).then_inc(wt_sb, 1)
            def prepare_w1():
                act.wait_ge(wt_ps, 3)
                act.activation(wofT[:, :, :], ps[:, 2, 0:2 * P], ACT.Copy)
                act.activation(wgh[:, :], ps[:, 2, 2 * P:2 * P + EXPERTS], ACT.Copy).then_inc(wt_sb, 1)
                for e in range(EXPERTS):
                    act.wait_ge(w1_ps, e + 1)
                    act.activation(w1h[:, e, :], ps[:, W1B[e % 3], :], ACT.Copy).then_inc(w1_hi, 1)

            def stage(name, n, i):
                f0, l1 = ps[:, F0, :], ps[:, L1, :]
                if name == "F_ctx":
                    act.wait_ge(ctxT_ps, at(i, 1, 1))
                    act.activation(ctxT[:, :], f0[:, 0:TOK], ACT.Copy)
                    act.activation(ctx2[:, :, :, :], spread(f0[:, 0:TOK].rearrange("p (b a t) -> p b a t", b=BPG, a=1),
                                                            2, 2), ACT.Copy).then_inc(ctxT_sb, 1)
                if name == "F_k":
                    act.wait_ge(kT_ps, at(i, 1, 1))
                    wait(act, kbd_sb, at(i, BPG, 0))
                    act.activation(kT[:, :], f0[:, TOK:2 * TOK], ACT.Copy).then_inc(kT_sb, 1)
                if name == "F_T":
                    act.wait_ge(xnT_ps["F"], at(i, 1, 1))
                    act.activation(xnT[:, :], f0[:, 0:TOK], ACT.Copy).then_inc(xnT_sb, 1)
                if name == "F_q":
                    act.wait_ge(cleared, 3)
                    act.wait_ge(qT_ps, at(i, 1, 1))
                    for g in range(ROWG):
                        rows = slice(32 * g, 32 * g + 32)
                        act.activation(qm[rows, :, g % 2, g // 2, :],
                                       ps[rows, F0, TOK:2 * TOK].rearrange("p (b t) -> p b t", b=BPG),
                                       ACT.Copy).then_inc(qm_sb, 1)
                if name == "F_v":
                    act.wait_ge(vx_ones, 2)
                    act.wait_ge(v_ps, at(i, 1, 1))
                    for m in range(2):
                        half = slice(SEQ * m, SEQ * m + SEQ)
                        act.activation(v_half(vxh, half, m), v_src(half, m), ACT.Copy).then_inc(v_hi, 1)
                if name == "S":
                    act.wait_ge(s_sub, at(i, UNITS, n + 1))
                    wait(act, pT_ps, at(i, UNITS, n - 1))
                    act.activation(prob[:, n % 2, :], ssub[:, n % 2, :], ACT.Exp, scale=SCALE0).then_inc(p_sb, 1)
                if name == "T":
                    act.wait_ge(pT_ps, at(i, UNITS, n + 1))
                    wait(act, o_ps, at(i, UNITS, n - 1))
                    act.activation(ph[:, n % 2, :, :], ps[:, PT, :], ACT.Copy).then_inc(p_hi, 1)
                if name == "O":
                    act.wait_ge(oT_ps, at(i, TILES, n + 1))
                    for g in range(2):
                        for b in range(2):
                            act.activation(oT[SEQ * g:SEQ * g + SEQ, n % 2, SEQ * b:SEQ * b + SEQ],
                                           ps[SEQ * b:SEQ * b + SEQ, AO, 384 + SEQ * g:384 + SEQ * g + SEQ],
                                           ACT.Copy).then_inc(oT_sb, 1)
                if name == "B_T":
                    act.wait_ge(xnT_ps["B"], at(i, 1, 1))
                    act.activation(xh[:, :], ps[:, HB, 0:TOK], ACT.Copy).then_inc(xh_sb, 1)
                if name == "B_gate":
                    act.wait_ge(ls_sb, at(i, 1, 1))
                    act.activation(ge[:, :, :], ls[:, :, :], ACT.Exp).then_inc(ge_sb, 1)
                if name == "E":
                    t, e = divmod(n, EXPERTS)
                    act.wait_ge(h_ps, at(i, EXP, n + 1))
                    act.activation(th[:, n % GATES, :], ps[:, HB + n % 2, HID:UP], ACT.Tanh,
                                   scale=0.5).then_inc(th_sb, 1)
                    act.wait_ge(comb_sb, at(i, 1, 1))
                    wait(act, g_sb, at(i, EXP, n + 1 - GATES))
                    act.wait_ge(th_sb, at(i, EXP, n + 1))
                    act.activation(sg[:, n % GATES, :], th[:, n % GATES, :], ACT.Identity, scale=comb[:, t, e:e + 1],
                                   bias=comb[:, t, e:e + 1]).then_inc(sg_sb, 1)
                if name == "G":
                    act.wait_ge(gT_ps, at(i, TILES, n + 1))
                    wait(act, y1_ps, at(i, TILES, n - 1))
                    act.activation(gT[:, n % 2, :, :], f0[:, 0:2 * P], ACT.Copy).then_inc(gT_sb, 1)
                if name == "C_T":
                    act.wait_ge(xnT_ps["C"], at(i, 1, 1))
                    act.activation(cx[:, :], l1, ACT.Copy).then_inc(cx_sb, 1)
                if name == "C_q":
                    act.wait_ge(kq_ps, at(i, 1, 1))
                    act.activation(kq[:, :], l1, ACT.Copy).then_inc(kq_sb, 1)
                if name == "C_s":
                    act.wait_ge(s1_ps, at(i, 1, 1))
                    act.activation(v1[:, :, :], l1[:, TOK:2 * TOK], ACT.Copy).then_inc(v1_sb, 1)
                if name == "C_p":
                    act.wait_ge(nb1_sb, at(i, 1, 1))
                    for t in range(TILES):
                        act.activation(p1[:, t, :], sm1[:, t, :], ACT.Exp, scale=SCALE1, bias=nb1[:, t:t + 1],
                                       accum_out=den1[:, t:t + 1]).then_inc(p1_sb, 1)
                    act.wait_ge(p1T_ps, at(i, 1, 1))
                    act.activation(p1T[:, :, :], l1[:, 0:TOK], ACT.Copy).then_inc(p1T_sb, 1)
                if name == "C_out":
                    act.wait_ge(xo_sb, at(i, 1, 1))
                    act.dma_start(out_dram[:, bass.ts(i, TILES), :], xout[:, :, :]).then_inc(xout_free, 16)
                if name == "C_x4":
                    act.wait_ge(cleared, 4)
                    act.wait_ge(xnT_ps["D"], at(i, 1, 1))
                    act.activation(x4p[:, :, 1:SEQ + 1], l1[:, 0:TOK].rearrange("p (b t) -> p b t", b=BPG),
                                   ACT.Copy).then_inc(x4_sb, 1)
                if name == "C_kr":
                    act.wait_ge(kr_ps, at(i, 1, 1))
                    act.activation(krelu[:, :], l1[:, 0:TOK], ACT.Relu).then_inc(krelu_sb, 1)
                    act.activation(thr[:, :], l1[:, TOK:2 * TOK], ACT.Tanh, scale=0.5).then_inc(thr_sb, 1)
                    act.wait_ge(krelu_sb, at(i, 1, 1))
                    act.activation(kact[:, :], krelu[:, :], ACT.Square).then_inc(kact_sb, 1)

            steps(act, ACT_ORDER, stage, prepare_w1)

        @block.vector
        def _(dve):
            dve.memset(vxh[:, :, :, :, :, :], 0.0).then_inc(cleared, 1)
            dve.memset(vxl[:, :, :, :, :, :], 0.0).then_inc(cleared, 1)
            dve.memset(qm[:, :, :, :, :], 0.0).then_inc(cleared, 1)
            dve.memset(x4p[:, :, 0:1], 0.0).then_inc(cleared, 1)
            dve.memset(xout[:, 0:1, 0:1], 0.0).then_inc(xout_free, 16)
            dve.wait_ge(cleared, 1)
            for m in range(2):
                dve.memset(vxh[SEQ * m:SEQ * m + SEQ, :, :, :, m, HD:HD + 1], 1.0).then_inc(vx_ones, 1)
            dve.wait_ge(ld_mu, 32)
            dve.tensor_scalar(omu[:, :], mu[:, :], -1.0, 1.0, ALU.mult, ALU.add).then_inc(omu_s, 1)

            def prepare_w1():
                dve.wait_ge(ld_wg, 16)
                dve.tensor_scalar(wg_nat[:, 0:D - 1], wg_nat[:, 0:D - 1], wg_nat[:, D - 1:D], None,
                                  ALU.subtract).then_inc(wg_adj, 1)
                dve.wait_ge(wg_adj, 1)
                dve.memset(wg_nat[:, D - 1:D], 0.0).then_inc(wg_adj, 1)
                dve.wait_ge(ld_w1, 16)
                for c in range(4):
                    rows = slice(c * W1CH // 4, (c + 1) * W1CH // 4)
                    dve.tensor_tensor(w1_nat[:, rows, 0:D - 1], w1_nat[:, rows, 0:D - 1],
                                      spread(w1_nat[:, rows, D - 1:D], 2, D - 1), ALU.subtract).then_inc(w1_sub, 1)
                dve.wait_ge(w1_sub, 4)
                dve.wait_ge(b1_ps, 1)
                dve.tensor_copy(w1_nat[:, :, D - 1], ps[:, 3, 0:W1CH]).then_inc(w1_adj, 1)
                dve.wait_ge(omu_s, 1)
                dve.wait_ge(wt_sb, 2)
                for r in range(2):
                    dve.tensor_scalar(wmix[:, r, 0, :], wT[:, WR + r, :], omu[:, r:r + 1], None, ALU.mult)
                    dve.tensor_scalar(wmix[:, r, 1, :], wT[:, WR + r, :], mu[:, r:r + 1], None,
                                      ALU.mult).then_inc(wmix_s, 1)
                dve.wait_ge(wt_sb, 3)
                dve.tensor_tensor(wgl[:, :], ps[:, 2, 2 * P:2 * P + EXPERTS], wgh[:, :], ALU.subtract).then_inc(wgl_s, 1)
                for e in range(EXPERTS):
                    dve.wait_ge(w1_hi, e + 1)
                    dve.tensor_tensor(w1l[:, e, :], ps[:, W1B[e % 3], :], w1h[:, e, :], ALU.subtract).then_inc(w1_lo, 1)

            count = dict.fromkeys(SETTLES, 0)

            def stage(name, n, i):
                phase = PHASE[name] if n is not None else name[0]

                def settle(ins, apart=False):
                    count[phase] = count[phase] % SETTLES[phase] + 1
                    ins.then_inc(settled[phase], 1)
                    dve.wait_ge(settled[phase], at(i, SETTLES[phase], count[phase]))
                    if apart:
                        dve.memset(spare[:, :], 0.0)

                def moments(ln, src):
                    for t in range(TILES):
                        done = dve.bn_stats(stats[ln][:, t, :], src[:, t, :])
                    settle(done, apart=True)
                    for t in range(TILES):
                        done = dve.bn_aggr(mv[ln][:, t, :], stats[ln][:, t, :])
                    done.then_inc(ln_var[ln], 1)

                def normed(ln, src, w=D):
                    dve.wait_ge(ln_rstd[ln], at(i, 1, 1))
                    wait(dve, xnT_ps[ln], at(i, 1, 0))
                    for t in range(TILES):
                        dve.tensor_scalar(xn[ln][:, t, 0:w], src[:, t, 0:w], mv[ln][:, t, 0:1], rstd[ln][:, t:t + 1],
                                          ALU.subtract, ALU.mult).then_inc(xn_sb[ln], 1)

                if name == "F_ln":
                    dve.wait_ge(xin_in, at(i, 16, 16))
                    moments("F", xin)
                if name == "F_T":
                    normed("F", xin)
                if name == "F_v":
                    dve.wait_ge(v_hi, at(i, 2, 2))
                    for m in range(2):
                        half = slice(SEQ * m, SEQ * m + SEQ)
                        dve.tensor_tensor(v_half(vxl, half, m), v_src(half, m), v_half(vxh, half, m),
                                          ALU.subtract).then_inc(v_lo, 1)
                if name == "S":
                    s3 = ps[:, SC + n % 2, :].rearrange("p (h c) -> p h c", c=SEQ)
                    dve.wait_ge(s_ps, at(i, UNITS, n + 1))
                    settle(dve.tensor_reduce(mx[:, n % 2, :], s3, AX.X, ALU.max))
                    wait(dve, p_sb, at(i, UNITS, n - 1))
                    dve.tensor_tensor(ssub[:, n % 2, :].rearrange("p (h c) -> p h c", c=SEQ), s3,
                                      spread(mx[:, n % 2, :].unsqueeze(2), 2, SEQ), ALU.subtract).then_inc(s_sub, 1)
                if name == "T":
                    dve.wait_ge(p_hi, at(i, UNITS, n + 1))
                    dve.tensor_tensor(pl[:, n % 2, :, :], ps[:, PT, :].rearrange("p (c t) -> p c t", c=4),
                                      ph[:, n % 2, :, :], ALU.subtract).then_inc(p_lo, 1)
                if name == "O":
                    dve.wait_ge(o_ps, at(i, UNITS, 2 * n + 2))
                    o = ps[:, AO, 0:288].rearrange("p (b g h w) -> p b g h w", b=2, g=2, w=HD + 1)
                    for g in range(2):
                        half = slice(SEQ * g, SEQ * g + SEQ)
                        done = dve.reciprocal(rden[half, :, :], o[half, :, g, :, HD])
                    settle(done)
                    wait(dve, oT_ps, at(i, TILES, n - 1))
                    for g in range(2):
                        half = slice(SEQ * g, SEQ * g + SEQ)
                        dve.tensor_tensor(onorm[half, n % 2, :].rearrange("p (b h d) -> p b h d", b=2, d=HD),
                                          o[half, :, g, :, 0:HD],
                                          spread(rden[half, :, :].unsqueeze(3), 3, HD), ALU.mult).then_inc(o_nrm, 1)
                if name == "Y":
                    dve.wait_ge(xb_sb, at(i, 1, 1))
                    dve.wait_ge(y0_ps, at(i, TILES, n + 1))
                    dve.tensor_tensor(x1[:, n, :], ps[:, AO, 0:P], xb[:, n, :], ALU.add).then_inc(x1_sb, 1)
                if name == "B_ln":
                    dve.wait_ge(x1_sb, at(i, TILES, TILES))
                    moments("B", x1)
                if name == "B_T":
                    wait(dve, xnT_ps["B"], at(i, 1, 0))
                    dve.memset(xn["B"][:, :, D - 1:D], 1.0)
                    normed("B", x1, D - 1)
                    dve.wait_ge(xh_sb, at(i, 1, 1))
                    dve.tensor_tensor(xl[:, :], ps[:, HB, 0:TOK], xh[:, :], ALU.subtract).then_inc(xl_sb, 1)
                if name == "B_gate":
                    dve.wait_ge(lg_ps, at(i, 1, 1))
                    settle(dve.tensor_copy(lg[:, :, :], ps[:, HB + 1, 0:TILES * EXPERTS]), apart=True)
                    for t in range(TILES):
                        done = dve.max(top[:, t, :], lg[:, t, :])
                    settle(done)
                    dve.tensor_tensor(ls[:, :, :], lg[:, :, :], spread(top[:, :, 0:1], 2, EXPERTS),
                                      ALU.subtract).then_inc(ls_sb, 1)
                    for t in range(TILES):
                        done = dve.max_index(topi[:, t, :], top[:, t, :], lg[:, t, :])
                    settle(done)
                    settle(dve.tensor_copy(topf[:, :, :], topi[:, :, 0:2]))
                    ie = spread(iota_e[:, :].unsqueeze(1), 1, TILES)
                    dve.wait_ge(c_iota, 2)
                    dve.tensor_tensor(sel0[:, :, :], ie, spread(topf[:, :, 0:1], 2, EXPERTS), ALU.is_equal)
                    settle(dve.tensor_tensor(sel1[:, :, :], ie, spread(topf[:, :, 1:2], 2, EXPERTS), ALU.is_equal))
                    settle(dve.tensor_tensor(sel0[:, :, :], sel0[:, :, :], sel1[:, :, :], ALU.add))
                    dve.wait_ge(ge_sb, at(i, 1, 1))
                    dve.tensor_reduce(zsum[:, :], ge[:, :, :], AX.X, ALU.add)
                    settle(dve.tensor_tensor(es[:, :, :], ge[:, :, :], sel0[:, :, :], ALU.mult))
                    settle(dve.tensor_reduce(ssum[:, :], es[:, :, :], AX.X, ALU.add))
                    settle(dve.scalar_tensor_tensor(gden[:, :], zsum[:, :], EPS_GATE, ssum[:, :], ALU.mult, ALU.add))
                    settle(dve.reciprocal(gden[:, :], gden[:, :]))
                    dve.tensor_tensor(csum[:, :], ssum[:, :], gden[:, :], ALU.mult)
                    for t in range(TILES):
                        done = dve.tensor_scalar(comb[:, t, :], es[:, t, :], gden[:, t:t + 1], 0.5, ALU.mult, ALU.mult)
                    done.then_inc(comb_sb, 1)
                    dve.wait_ge(comb_sb, at(i, 1, 1))
                    dve.wait_ge(ld_bof, 16)
                    for t in range(TILES):
                        done = dve.scalar_tensor_tensor(xB[:, t, :], bof[:, :], csum[:, t:t + 1], x1[:, t, :],
                                                        ALU.mult, ALU.add)
                    settle(done)
                if name == "E":
                    t, e = divmod(n, EXPERTS)
                    dve.wait_ge(sg_sb, at(i, EXP, n + 1))
                    if e < POOL_E:
                        m = t * POOL_E + e
                        g_out = gb[:, m % GBUF, :]
                        mt, me = divmod(m - GBUF, POOL_E)
                        wait(dve, acc_pool, at(i, ADDS, mt * (POOL_E - 1) + max(me, 1)))
                    else:
                        g_out = g67[:, e - POOL_E, :]
                    dve.tensor_tensor(g_out, ps[:, HB + n % 2, 0:HID], sg[:, n % GATES, :], ALU.mult).then_inc(g_sb, 1)
                    if e == EXPERTS - 1:
                        dve.wait_ge(g_sb, at(i, EXP, n + 1))
                        wait(dve, gT_ps, at(i, TILES, t - 1))
                        settle(dve.tensor_tensor(accd[:, t % 2, :], g67[:, 0, :], g67[:, 1, :], ALU.add))
                if name == "G":
                    dve.wait_ge(acc_pool, at(i, ADDS, (n + 1) * (POOL_E - 1)))
                    dve.tensor_tensor(accd[:, n % 2, :], accd[:, n % 2, :], accp[:, n % 2, :],
                                      ALU.add).then_inc(acc_sb, 1)
                if name == "H":
                    dve.wait_ge(y1_ps, at(i, TILES, n + 1))
                    dve.tensor_tensor(x2[:, n, :], ps[:, F0, 2 * P:3 * P], xB[:, n, :], ALU.add).then_inc(x2_sb, 1)
                if name == "C_ln":
                    dve.wait_ge(x2_sb, at(i, TILES, TILES))
                    moments("C", x2)
                if name == "C_T":
                    normed("C", x2)
                if name == "C_s":
                    dve.wait_ge(v1_sb, at(i, 1, 1))
                    dve.wait_ge(c_cau, 3)
                    settle(dve.tensor_tensor(sm1[:, :, :], ps[:, L1, 0:TOK].rearrange("p (n c) -> p n c", c=P),
                                             spread(causal[:, :].unsqueeze(1), 1, TILES), ALU.add))
                    settle(dve.tensor_reduce(mx1[:, :], sm1[:, :, :], AX.X, ALU.max))
                    dve.tensor_scalar(nb1[:, :], mx1[:, :], -SCALE1, None, ALU.mult).then_inc(nb1_sb, 1)
                if name == "C_y":
                    dve.wait_ge(p1_sb, at(i, TILES, TILES))
                    settle(dve.reciprocal(rd1[:, :], den1[:, :]))
                    dve.wait_ge(y2_ps, at(i, 1, 1))
                    for t in range(TILES):
                        done = dve.scalar_tensor_tensor(x3[:, t, :], ps[:, L1, TOK + t * P:TOK + (t + 1) * P],
                                                        rd1[:, t:t + 1], x2[:, t, :], ALU.mult, ALU.add)
                    settle(done)
                if name == "C_ln4":
                    moments("D", x3)
                if name == "C_x4":
                    normed("D", x3)
                if name == "C_v":
                    dve.wait_ge(thr_sb, at(i, 1, 1))
                    dve.wait_ge(vf_ps, at(i, 1, 1))
                    dve.scalar_tensor_tensor(uu[:, :], thr[:, :], 1.0, ps[:, L1, 0:TOK], ALU.add,
                                             ALU.mult).then_inc(u_sb, 1)
                if name == "C_u":
                    dve.wait_ge(uT_ps, at(i, 1, 1))
                    dve.wait_ge(xout_free, at(i, 16, 16))
                    dve.scalar_tensor_tensor(xout[:, :, :], ps[:, L1, TOK:2 * TOK].rearrange("p (n d) -> p n d", d=D),
                                             0.5, x3[:, :, :], ALU.mult, ALU.add).then_inc(xo_sb, 1)

            steps(dve, DVE_ORDER, stage, prepare_w1)
            assert count == SETTLES, count

        @block.tensor
        def _(pe):
            pe.wait_ge(c_ident, 1)
            pe.wait_ge(ld_sq, 16 * SQ)
            for n in range(SQ):
                done = pe.transpose(ps[:, n // 4, bass.ts(n % 4, P)], w_nat[:, n, :], ident[:, :])
                if n % 4 == 3:
                    done.then_inc(wt_ps, 1)
            pe.wait_ge(vx_ones, 2)
            pe.wait_ge(wt_sb, 2)

            def prepare_w1():
                pe.wait_ge(ld_small, 32)
                pe.wait_ge(wg_adj, 2)
                for j in range(2):
                    pe.transpose(ps[:, 2, bass.ts(j, P)], wof_nat[:, j, :], ident[:, :])
                pe.transpose(ps[:, 2, 2 * P:2 * P + EXPERTS], wg_nat[:, :], ident[0:EXPERTS, 0:EXPERTS]).then_inc(wt_ps, 1)
                pe.transpose(ps[:, 3, 0:W1CH], b1_nat[:, :], ident[0:W1CH, 0:W1CH]).then_inc(b1_ps, 1)
                pe.wait_ge(w1_adj, 1)
                for e in range(EXPERTS):
                    if e >= 3:
                        pe.wait_ge(w1_lo, e - 2)
                    for j in range(4):
                        done = pe.transpose(ps[:, W1B[e % 3], bass.ts(j, P)], w1_nat[:, 4 * e + j, :], ident[:, :])
                    done.then_inc(w1_ps, 1)
                pe.wait_ge(wgl_s, 1)
                pe.wait_ge(w1_lo, EXPERTS)
                pe.wait_ge(wmix_s, 2)

            def turn(ln, i, bank, at_col):
                for t in range(TILES):
                    pe.wait_ge(xn_sb[ln], at(i, TILES, t + 1))
                    done = pe.transpose(ps[:, bank, at_col + t * P:at_col + (t + 1) * P], xn[ln][:, t, :], ident[:, :])
                done.then_inc(xnT_ps[ln], 1)

            def stage(name, n, i):
                f0, l1 = ps[:, F0, :], ps[:, L1, :]
                if name == "F_ctx":
                    wait(pe, x2_sb, at(i - 2, TILES, 0))
                    wait(pe, v_lo, at(i, 2, 0))
                    pe.wait_ge(cin_in, at(i, 16, 16))
                    for t in range(TILES):
                        done = pe.transpose(f0[:, bass.ts(t, P)], cin[:, t, :], ident[:, :])
                    done.then_inc(ctxT_ps, 1)
                if name == "F_k":
                    pe.wait_ge(ctxT_sb, at(i, 1, 1))
                    pe.matmul(f0[:, TOK:2 * TOK], wT[:, WK0, :], ctxT[:, :], start=True, stop=True).then_inc(kT_ps, 1)
                if name == "F_T":
                    pe.wait_ge(kT_sb, at(i, 1, 1))
                    turn("F", i, F0, 0)
                if name == "F_q":
                    pe.wait_ge(xnT_sb, at(i, 1, 1))
                    pe.matmul(f0[:, TOK:2 * TOK], wT[:, WQ0, :], xnT[:, :], start=True, stop=True).then_inc(qT_ps, 1)
                if name == "F_v":
                    pe.wait_ge(qm_sb, at(i, ROWG, ROWG))
                    wait(pe, x2_sb, at(i - 2, TILES, 1))
                    for b in range(BPG):
                        done = pe.matmul(f0[:, bass.ts(b, P)], ctx2[:, b, :, :], wT[:, WV0, :], start=True, stop=True)
                    done.then_inc(v_ps, 1)
                if name == "S":
                    pe.wait_ge(qm_sb, at(i, ROWG, ROWG))
                    pe.wait_ge(kbd_sb, at(i, BPG, n + 1))
                    wait(pe, s_sub, at(i, UNITS, n - 1))
                    for g in range(2):
                        done = pe.matmul(ps[:, SC + n % 2, 256 * g:256 * g + 256], qm[:, n, g, :, :], kbd[:, n, :, :],
                                         start=True, stop=True)
                    done.then_inc(s_ps, 1)
                if name == "T":
                    pe.wait_ge(p_sb, at(i, UNITS, n + 1))
                    wait(pe, p_lo, at(i, UNITS, n))
                    for c in range(4):
                        done = pe.transpose(ps[:, PT, bass.ts(c, P)], prob[:, n % 2, bass.ts(c, P)], ident[:, :])
                    done.then_inc(pT_ps, 1)
                if name == "V":
                    t, b = divmod(n, 2)
                    if n == 0:
                        pe.wait_ge(v_lo, at(i, 2, 2))
                    if b == 0:
                        wait(pe, x1_sb, at(i, TILES, t))
                    pe.wait_ge(p_lo, at(i, UNITS, n + 1))
                    for c in range(4):
                        o = ps[:, AO, 0:288].rearrange("p (b g h w) -> p b g h w", b=2, g=2, h=4)[:, b, :, c, :]
                        vh = vxh[:, n, :, c, :, :].rearrange("p g m w -> p g (m w)")
                        vl = vxl[:, n, :, c, :, :].rearrange("p g m w -> p g (m w)")
                        pe.matmul(o, ph[:, n % 2, c, :], vh, start=True, stop=False)
                        pe.matmul(o, ph[:, n % 2, c, :], vl, start=False, stop=False)
                        done = pe.matmul(o, pl[:, n % 2, c, :], vh, start=False, stop=True)
                    done.then_inc(o_ps, 1)
                if name == "O":
                    pe.wait_ge(o_nrm, at(i, 2 * TILES, 2 * n + 2))
                    pe.transpose(ps[:, AO, 384:512], onorm[:, n % 2, :], ident[:, :]).then_inc(oT_ps, 1)
                if name == "Y":
                    pe.wait_ge(oT_sb, at(i, 4 * TILES, 4 * n + 4))
                    pe.matmul(ps[:, AO, 0:P], oT[:, n % 2, :], wT[:, WO0, :], start=True, stop=True).then_inc(y0_ps, 1)
                if name == "B_T":
                    wait(pe, g_sb, at(i, EXP, -1))
                    turn("B", i, HB, 0)
                if name == "B_gate":
                    wait(pe, g_sb, at(i, EXP, 0))
                    pe.wait_ge(xh_sb, at(i, 1, 1))
                    pe.wait_ge(xl_sb, at(i, 1, 1))
                    for t in range(TILES):
                        o = ps[:, HB + 1, EXPERTS * t:EXPERTS * t + EXPERTS]
                        pe.matmul(o, xh[:, bass.ts(t, P)], wgh[:, :], start=True, stop=False)
                        pe.matmul(o, xh[:, bass.ts(t, P)], wgl[:, :], start=False, stop=False)
                        done = pe.matmul(o, xl[:, bass.ts(t, P)], wgh[:, :], start=False, stop=True)
                    done.then_inc(lg_ps, 1)
                if name == "E":
                    t, e = divmod(n, EXPERTS)
                    o = ps[:, HB + n % 2, :]
                    wait(pe, g_sb, at(i, EXP, n - 1))
                    if n == 1:
                        pe.wait_ge(ls_sb, at(i, 1, 1))
                    pe.matmul(o, xh[:, bass.ts(t, P)], w1h[:, e, :], start=True, stop=False)
                    pe.matmul(o, xh[:, bass.ts(t, P)], w1l[:, e, :], start=False, stop=False)
                    pe.matmul(o, xl[:, bass.ts(t, P)], w1h[:, e, :], start=False, stop=True).then_inc(h_ps, 1)
                if name == "G":
                    if not isinstance(i, int) or i + 2 < GROUPS:
                        if n == 0:
                            pe.wait_ge(qm_sb, at(i + 2, ROWG, ROWG))
                        else:
                            pe.wait_ge(v_lo, at(i + 2, 2, 2))
                    wait(pe, x2_sb, at(i, TILES, n))
                    pe.wait_ge(acc_sb, at(i, TILES, n + 1))
                    for j in range(2):
                        done = pe.transpose(f0[:, bass.ts(j, P)], accd[:, n % 2, bass.ts(j, P)], ident[:, :])
                    done.then_inc(gT_ps, 1)
                if name == "H":
                    pe.wait_ge(gT_sb, at(i, TILES, n + 1))
                    for j in range(2):
                        done = pe.matmul(f0[:, 2 * P:3 * P], gT[:, n % 2, j, :], wofT[:, j, :],
                                         start=(j == 0), stop=(j == 1))
                    done.then_inc(y1_ps, 1)
                if name == "C_ctx":
                    wait(pe, xo_sb, at(i, 1, 0))
                    pe.wait_ge(cinc_in, at(i, 16, 16))
                    for t in range(TILES):
                        done = pe.transpose(l1[:, bass.ts(t, P)], cinc[:, t, :], ident[:, :])
                    done.then_inc(cc_ps, 1)
                if name == "C_T":
                    turn("C", i, L1, TOK)
                if name == "C_q":
                    pe.wait_ge(cx_sb, at(i, 1, 1))
                    pe.matmul(l1, wT[:, WQ1, :], cx[:, :], start=True, stop=True).then_inc(kq_ps, 1)
                if name == "C_s":
                    pe.wait_ge(kq_sb, at(i, 1, 1))
                    for t in range(TILES):
                        pe.matmul(l1[:, bass.ts(t, P)], kq[:, TOK + t * P:TOK + (t + 1) * P], kq[:, bass.ts(t, P)],
                                  start=True, stop=True)
                        done = pe.matmul(l1[:, TOK + t * P:TOK + (t + 1) * P], cx[:, bass.ts(t, P)], wT[:, WQ1, :],
                                         start=True, stop=True)
                    done.then_inc(s1_ps, 1)
                if name == "C_p":
                    for t in range(TILES):
                        pe.wait_ge(p1_sb, at(i, TILES, t + 1))
                        done = pe.transpose(l1[:, bass.ts(t, P)], p1[:, t, :], ident[:, :])
                    done.then_inc(p1T_ps, 1)
                if name == "C_y":
                    pe.wait_ge(p1T_sb, at(i, 1, 1))
                    for t in range(TILES):
                        done = pe.matmul(l1[:, TOK + t * P:TOK + (t + 1) * P], p1T[:, t, :], v1[:, t, :],
                                         start=True, stop=True)
                    done.then_inc(y2_ps, 1)
                if name == "C_x4":
                    turn("D", i, L1, 0)
                if name == "C_kr":
                    pe.wait_ge(x4_sb, at(i, 1, 1))
                    for r, o in ((1, l1[:, 0:TOK]), (0, l1[:, TOK:2 * TOK])):
                        pe.matmul(o, wmix[:, r, 0, :], x4p[:, :, 0:SEQ], start=True, stop=False)
                        done = pe.matmul(o, wmix[:, r, 1, :], x4p[:, :, 1:SEQ + 1], start=False, stop=True)
                    done.then_inc(kr_ps, 1)
                if name == "C_v":
                    pe.wait_ge(kact_sb, at(i, 1, 1))
                    pe.matmul(l1[:, 0:TOK], wT[:, WVF, :], kact[:, :], start=True, stop=True).then_inc(vf_ps, 1)
                if name == "C_u":
                    pe.wait_ge(u_sb, at(i, 1, 1))
                    for t in range(TILES):
                        done = pe.transpose(l1[:, TOK + t * P:TOK + (t + 1) * P], uu[:, bass.ts(t, P)], ident[:, :])
                    done.then_inc(uT_ps, 1)

            steps(pe, PE_ORDER, stage, prepare_w1)
    return nc


_INS = ['x', 'ctx_1024', 'L0_xattn_Wq', 'L0_xattn_Wk', 'L0_xattn_Wv', 'L0_xattn_Wo', 'L0_xattn_bo', 'L0_ffn_Wg',
        'L0_ffn_W1', 'L0_ffn_b1', 'L0_ffn_Wo', 'L0_ffn_bo', 'L1_xattn_Wq', 'L1_ffn_W_r', 'L1_ffn_W_k', 'L1_ffn_W_v',
        'L1_ffn_mu_r', 'L1_ffn_mu_k']


def kernel(**inputs):
    import numpy as _np
    import concourse.bacc as _bacc
    from concourse.bass_utils import run_bass_kernel_spmd as _run

    nc = _bacc.Bacc("TRN2", target_bir_lowering=False, num_devices=1)
    arrays, args = {}, []
    for name in _INS:
        a = _np.ascontiguousarray(inputs[name])
        arrays[f"in_{name}"] = a
        args.append(nc.dram_tensor(f"in_{name}", a.shape, mybir.dt.from_np(a.dtype), kind="ExternalInput").ap())
    args.append(nc.dram_tensor("out_x", (BATCH, SEQ, D), F32, kind="ExternalOutput").ap())
    build(nc, *args)
    r = _run(nc, [arrays], core_ids=[0])
    return r.results[0]["out_x"]
```

```python
import concourse.bass as bass
from concourse import mybir
from contextlib import ExitStack

F32 = mybir.dt.float32
F16 = mybir.dt.float16
U32 = mybir.dt.uint32
ALU = mybir.AluOpType
ACT = mybir.ActivationFunctionType
AX = mybir.AxisListType

P = 128
BATCH, SEQ, D = 32, 64, 128
HEADS = 16
HD = D // HEADS
PAIRS = HEADS // 2
ROWG = 4
HPG = HEADS // ROWG
EXPERTS, HID = 8, 256
UP = 2 * HID
TILES = 2
BPG = 2 * TILES
TOK = TILES * P
GROUPS = BATCH * SEQ // TOK
UNITS = BPG
GATES = 4
GBUF = 4
EPS_LN = 1e-5
EPS_GATE = 1e-9
SCALE0 = float(D) ** -0.5
SCALE1 = float(D) ** -0.5
NEG = -1e30

SC, PT, AO, HB, L1, F0 = 0, 2, 3, 4, 6, 7

PE_ORDER = (
    """S2+1 H0+2 E14+2 E15+2 C_x4+2 T0+1 W3+2 F_v+2 B_T+1 C_kr+2 W4+2 T1+1 B_gate+1 E0+1 W5+2 E1+1 S3+1 G1+2 V0+1 E2+1
    C_v+2 H1+2 W6+2 W7+2 T2+1 E3+1 F_ctx+1 E4+1 W_qkv+1 C_u+2 V1+1 E5+1 F_k+1 C_ctx+1 E6+1 C_T+1 O0+1 F_T+1 E7+1
    C_q+1 W_sq+1 Y0+1 E8+1 T3+1 E9+1 C_s+1 F_q+1 E10+1 V2+1 V3+1 E11+1 S0 O1+1 C_p+1 S1 C_y+1 E12+1 W_small+1 Y1+1
    W0+1 G0+1 W1+1 E13+1 W2+1""".split(),
    """T0+1 H0+2 E14+2 F_v+2 E15+2 C_x4+2 S2+1 B_T+1 C_kr+2 B_gate+1 E0+1 E1+1 G1+2 C_v+2 T1+1 H1+2 E2+1 V0+1 F_ctx+1
    C_u+2 E3+1 S3+1 F_k+1 C_ctx+1 T2+1 V1+1 C_T+1 E4+1 E5+1 F_T+1 C_q+1 E6+1 O0+1 E7+1 C_s+1 F_q+1 E8+1 Y0+1 T3+1
    E9+1 S0 C_p+1 V2+1 V3+1 E10+1 C_y+1 E11+1 O1+1 S1 E12+1 Y1+1 G0+1 E13+1""".split(),
    """T0+1 E14+2 H0+2 S2+1 C_x4+2 E15+2 F_v+2 B_T+1 C_kr+2 B_gate+1 E0+1 T1+1 G1+2 E1+1 C_v+2 H1+2 V0+1 E2+1 C_u+2
    F_ctx+1 E3+1 S3+1 C_ctx+1 E4+1 C_T+1 F_k+1 T2+1 V1+1 E5+1 C_q+1 E6+1 F_T+1 E7+1 C_s+1 O0+1 E8+1 T3+1 F_q+1 E9+1
    Y0+1 E10+1 V2+1 V3+1 S0 C_p+1 E11+1 O1+1 C_y+1 S1 E12+1 Y1+1 E13+1 G0+1""".split(),
)
ACT_ORDER = (
    """U12+2 G0+2 U13+2 E11+2 E12+2 W2+2 U14+2 S1+1 U15+2 C_x4+2 T0+1 B_T+1 E13+2 F_v+2 W3+2 W4+2 E14+2 E15+2 C_kr+2
    U0+1 C_sq+2 W5+2 U1+1 T1+1 B_gate+1 S2+1 W6+2 G1+2 W7+2 U2+1 T2+1 U3+1 F_ctx+1 E0+1 W_qkv+1 U4+1 E1+1 E2+1 U5+1
    F_k+1 C_out+2 E3+1 U6+1 C_T+1 O0+1 S3+1 U7+1 E4+1 F_T+1 C_q+1 U8+1 E5+1 T3+1 U9+1 E6+1 C_s+1 W_sq+1 F_q+1
    W_small+1 U10+1 C_p+1 U11+1 E7+1 C_pT+1 O1+1 W0+1 E8+1 W1+1 E9+1 E10+1 S0""".split(),
    """U12+2 G0+2 E11+2 U13+2 E12+2 T0+1 U14+2 E13+2 F_v+2 C_x4+2 U15+2 B_T+1 E14+2 E15+2 C_kr+2 C_sq+2 S1+1 U0+1 G1+2
    B_gate+1 U1+1 T1+1 S2+1 U2+1 F_ctx+1 C_out+2 U3+1 E0+1 E1+1 E2+1 F_k+1 E3+1 C_T+1 U4+1 T2+1 U5+1 E4+1 F_T+1
    C_q+1 O0+1 U6+1 U7+1 S3+1 C_s+1 F_q+1 U8+1 T3+1 C_p+1 E5+1 C_pT+1 U9+1 E6+1 U10+1 E7+1 E8+1 U11+1 O1+1 E9+1
    E10+1 S0""".split(),
    """U12+2 E11+2 U13+2 G0+2 E12+2 U14+2 T0+1 E13+2 S1+1 C_x4+2 E14+2 U15+2 B_T+1 F_v+2 E15+2 C_kr+2 U0+1 C_sq+2 G1+2
    U1+1 B_gate+1 S2+1 U2+1 F_ctx+1 T1+1 U3+1 C_out+2 E0+1 E1+1 U4+1 C_T+1 E2+1 T2+1 E3+1 F_k+1 U5+1 S3+1 C_q+1 U6+1
    E4+1 U7+1 E5+1 C_s+1 F_T+1 O0+1 U8+1 T3+1 F_q+1 U9+1 C_p+1 E6+1 U10+1 C_pT+1 E7+1 E8+1 E9+1 U11+1 O1+1 E10+1 S0""".split(),
)
DVE_ORDER = (
    """B_ln+1 C_ag4+2 E12+2 B_ag+1 E13+2 S1+1 C_x4+2 H0+2 B_T+1 E14+2 W2+2 M2+1 E15+2 T0+1 B_xl+1 S2+1 Q0+1 F_v+2 W3+2
    Q1+1 W4+2 Q2+1 E0+1 Q3+1 E1+1 Q4+1 T1+1 Q5+1 F_T+1 Q6+1 C_v+2 Q7+1 H1+2 Q8+1 E2+1 Q9+1 C_ln+1 Q10+1 E3+1 C_ag+1
    M3+1 C_u+2 E4+1 W_adj+1 R0+1 C_T+1 O0+1 E5+1 S3+1 E6+1 T2+1 E7+1 W5+2 Q11+1 F_ln E8+1 W6+2 Y0+1 T3+1 E9+1 W7+2
    C_s+1 W_sq+1 C_max+1 W_small+1 C_nb+1 R1+1 F_ag O1+1 E10+1 C_rd+1 M0 E11+1 S0 M1 W0+1 W1+1 C_y+1 Y1+1 C_ln4+1""".split(),
    """E12+2 C_ag4+2 B_ln+1 H0+2 B_ag+1 E13+2 C_x4+2 E14+2 B_T+1 S1+1 T0+1 E15+2 B_xl+1 F_v+2 Q0+1 Q1+1 M2+1 Q2+1 S2+1
    Q3+1 E0+1 Q4+1 C_v+2 Q5+1 H1+2 Q6+1 E1+1 Q7+1 C_ln+1 Q8+1 C_u+2 Q9+1 C_ag+1 Q10+1 T1+1 E2+1 C_T+1 E3+1 F_T+1
    Q11+1 R0+1 E4+1 O0+1 E5+1 M3+1 F_ln S3+1 E6+1 T2+1 C_s+1 E7+1 C_max+1 C_nb+1 F_ag E8+1 Y0+1 T3+1 C_rd+1 M0 R1+1
    E9+1 O1+1 E10+1 C_y+1 S0 E11+1 C_ln4+1 M1 Y1+1""".split(),
    """C_ag4+2 E12+2 B_ln+1 E13+2 B_ag+1 C_x4+2 S1+1 H0+2 E14+2 B_T+1 M2+1 T0+1 E15+2 B_xl+1 F_v+2 Q0+1 Q1+1 Q2+1 Q3+1
    E0+1 Q4+1 S2+1 Q5+1 E1+1 C_v+2 H1+2 Q6+1 C_ln+1 Q7+1 C_ag+1 Q8+1 C_u+2 Q9+1 E2+1 Q10+1 C_T+1 T1+1 E3+1 M3+1 S3+1
    E4+1 F_T+1 R0+1 E5+1 F_ln T2+1 O0+1 E6+1 Q11+1 E7+1 C_s+1 C_max+1 C_nb+1 E8+1 T3+1 Y0+1 E9+1 R1+1 C_rd+1 O1+1 M0
    E10+1 S0 C_y+1 E11+1 F_ag M1 C_ln4+1 Y1+1""".split(),
)
POOL_ORDER = (
    """K0+2 K1+2 E2+2 K2+2 E3+2 K3+2 E4+2 E5+2 E6+2 E7+2 E9+2 C_ag4+2 B_ag+1 E10+2 E11+2 E12+2 F_ag+1 E13+2 E14+2 E15+2
    A_x+1 C_ag+1 E1+1""".split(),
    """K0+2 K1+2 E2+2 E3+2 E4+2 E5+2 E6+2 E7+2 K2+2 E9+2 E10+2 C_ag4+2 B_ag+1 E11+2 E12+2 E13+2 E14+2 E15+2 K3+2 F_ag+1
    C_ag+1 A_x+1 E1+1""".split(),
    """K0+2 E2+2 K1+2 E3+2 K2+2 E4+2 K3+2 E5+2 E6+2 E7+2 F_ag+1 E9+2 E10+2 C_ag4+2 E11+2 B_ag+1 A_x+1 E12+2 E13+2 E14+2
    E15+2 C_ag+1 E1+1""".split(),
)
SP_ORDER = (
    """F_ctx W_sq W_w1 A_x C_ln""".split(),
    """F_ctx A_x C_ln""".split(),
    """F_ctx A_x C_ln""".split(),
)
PHASES = "FABC"
LAG = 2
LOOP_FROM = len(PHASES) + LAG
PHASE = {"M": "A", "S": "A", "T": "A", "V": "A", "R": "A", "O": "A", "Y": "A", "U": "B", "E": "B", "G": "B", "H": "B",
         "Q": "B", "K": "F", "W": "F"}
VPARTS = 4
GATE_STEPS = 10


def spread(ap, axis, n):
    shape = list(ap.shape)
    assert shape[axis] == 1
    shape[axis] = n
    return ap.broadcast_to(shape)


def build(nc, x, ctx_1024, L0_xattn_Wq, L0_xattn_Wk, L0_xattn_Wv, L0_xattn_Wo, L0_xattn_bo,
          L0_ffn_Wg, L0_ffn_W1, L0_ffn_b1, L0_ffn_Wo, L0_ffn_bo, L1_xattn_Wq,
          L1_ffn_W_r, L1_ffn_W_k, L1_ffn_W_v, L1_ffn_mu_r, L1_ffn_mu_k, out):
    x_dram = x.rearrange("b s d -> (b s) d").rearrange("(n p) d -> p n d", p=P)
    ctx_dram = ctx_1024.rearrange("b s d -> (b s) d").rearrange("(n p) d -> p n d", p=P)
    out_dram = out.rearrange("b s d -> (b s) d").rearrange("(n p) d -> p n d", p=P)

    with ExitStack() as stack:
        def sb(name, shape, dt=F32):
            return stack.enter_context(nc.sbuf_tensor(name, shape, dt))

        def sem(name):
            return stack.enter_context(nc.semaphore(name))

        SQ = 8
        WQ0, WK0, WV0, WO0, WQ1, WR, WKF, WVF = range(SQ)
        w_nat = sb("w_nat", [P, SQ, D])
        w1_nat = sb("w1_nat", [P, EXPERTS * UP // P, D])
        wof_nat = sb("wof_nat", [P, 2, P])
        wg_nat = sb("wg_nat", [EXPERTS, D])
        b1_nat = sb("b1_nat", [EXPERTS * UP // P, P])
        bo0 = sb("bo0", [P, D])
        bof = sb("bof", [P, D])
        mu = sb("mu", [P, 2])
        wT = sb("wT", [P, SQ, D])
        wmix = sb("wmix", [P, 2, 2, D])
        omu = sb("omu", [P, 2])
        w1h = sb("w1h", [P, EXPERTS, UP], F16)
        w1l = sb("w1l", [P, EXPERTS, UP], F16)
        wofT = sb("wofT", [P, 2, D])
        wgh = sb("wgh", [P, EXPERTS], F16)
        wgl = sb("wgl", [P, EXPERTS], F16)
        ident = sb("ident", [P, P])
        headmask = sb("headmask", [P, HPG, SEQ])
        causal = sb("causal", [P, P])
        hm0 = sb("hm0", [P, 3, HPG])
        hm1 = sb("hm1", [P, ROWG, HPG])
        iota_e = sb("iota_e", [P, EXPERTS])
        iota_i = sb("iota_i", [P, EXPERTS], mybir.dt.int32)
        eps_t = sb("eps_t", [P, TILES])
        mhalf = sb("mhalf", [P, TILES])
        spare = sb("spare", [P, 5])
        warm = sb("warm", [P, 1])
        LN = "FBCD"
        stats = {n: sb("stats" + n, [P, TILES, 6]) for n in LN}
        mv = {n: sb("mv" + n, [P, TILES, 2]) for n in LN}
        vare = {n: sb("vare" + n, [P, TILES]) for n in LN}
        rstd = {n: sb("rstd" + n, [P, TILES]) for n in LN}
        xn = {n: sb("xn" + n, [P, TILES, D]) for n in LN}
        xin = sb("xin", [P, TILES, D])
        cin = sb("cin", [P, TILES, D])
        ctxT = sb("ctxT", [P, TOK])
        kT = sb("kT", [P, TOK])
        xnT = sb("xnT", [P, TOK])
        qm = sb("qm", [P, BPG, 2, 2, SEQ])
        kbd = sb("kbd", [P, BPG, HPG, SEQ])
        vxh = sb("vxh", [P, BPG, 2, 4, 2, HD + 1], F16)
        vxl = sb("vxl", [P, BPG, 2, 4, 2, HD + 1], F16)
        xa = sb("xa", [P, TILES, D])
        xb = sb("xb", [P, TILES, D])
        HS = HEADS * SEQ // 2
        mx = sb("mx", [P, 2, HS // SEQ])
        ssub = sb("ssub", [P, 2, HS])
        prob = sb("prob", [P, 2, HS])
        ph = sb("ph", [P, 2, 4, P], F16)
        pl = sb("pl", [P, 2, 4, P], F16)
        rden = sb("rden", [P, 2, HEADS // 2])
        onorm = sb("onorm", [P, 2, D])
        oT = sb("oT", [P, 2, P])
        x1 = sb("x1", [P, TILES, D])
        xh = sb("xh", [P, TOK], F16)
        xl = sb("xl", [P, TOK], F16)
        lg = sb("lg", [P, TILES, EXPERTS])
        top = sb("top", [P, TILES, 8])
        topi = sb("topi", [P, TILES, 8], U32)
        topf = sb("topf", [P, TILES, 2])
        ls = sb("ls", [P, TILES, EXPERTS])
        ge = sb("ge", [P, TILES, EXPERTS])
        sel0 = sb("sel0", [P, TILES, EXPERTS])
        sel1 = sb("sel1", [P, TILES, EXPERTS])
        es = sb("es", [P, TILES, EXPERTS])
        ssum = sb("ssum", [P, TILES])
        zsum = sb("zsum", [P, TILES])
        gden = sb("gden", [P, TILES])
        comb = sb("comb", [P, TILES, EXPERTS])
        csum = sb("csum", [P, TILES])
        xB = sb("xB", [P, TILES, D])
        th = sb("th", [P, GATES, HID])
        gb = sb("gb", [P, GATES, HID])
        wg = sb("wg", [P, GBUF, HID])
        accp = sb("accp", [P, 2, HID])
        gT = sb("gT", [P, 2, 2, P])
        x2 = sb("x2", [P, TILES, D])
        cinc = sb("cinc", [P, TILES, D])
        cx = sb("cx", [P, 2 * TOK])
        kq = sb("kq", [P, 2 * TOK])
        v1 = sb("v1", [P, TILES, D])
        sm1 = sb("sm1", [P, TILES, P])
        mx1 = sb("mx1", [P, TILES])
        nb1 = sb("nb1", [P, TILES])
        den1 = sb("den1", [P, TILES])
        rd1 = sb("rd1", [P, TILES])
        p1 = sb("p1", [P, TILES, P])
        p1T = sb("p1T", [P, TILES, P])
        x3 = sb("x3", [P, TILES, D])
        x4p = sb("x4p", [P, BPG, SEQ + 1])
        krelu = sb("krelu", [P, TOK])
        kact = sb("kact", [P, TOK])
        thr = sb("thr", [P, TOK])
        uu = sb("uu", [P, TOK])
        xout = sb("xout", [P, TILES, D])

        ps = stack.enter_context(nc.psum_tensor("ps", [P, 8, 512], F32))

        ld_sq = sem("ld_sq")
        warm_set = sem("warm_set")
        xB_sb = sem("xB_sb")
        csum_sb = sem("csum_sb")
        ld_qkv = sem("ld_qkv")
        ld_bo0 = sem("ld_bo0")
        ld_bof = sem("ld_bof")
        ld_wg = sem("ld_wg")
        ld_mu = sem("ld_mu")
        ld_w1 = sem("ld_w1")
        ld_small = sem("ld_small")
        c_id0 = sem("c_id0")
        c_ident = sem("c_ident")
        c_pow = sem("c_pow")
        c_hm = sem("c_hm")
        c_cau = sem("c_cau")
        c_iota = sem("c_iota")
        cleared = sem("cleared")
        vx_ones = sem("vx_ones")
        wt_ps = sem("wt_ps")
        wt_sb = sem("wt_sb")
        omu_s = sem("omu_s")
        wmix_s = sem("wmix_s")
        wgl_s = sem("wgl_s")
        w1_sub = sem("w1_sub")
        w1_adj = sem("w1_adj")
        wg_adj = sem("wg_adj")
        w1_ps = sem("w1_ps")
        w1_hi = sem("w1_hi")
        w1_lo = sem("w1_lo")
        own = {n: sem("own_" + n) for n in ("lnF", "lnB", "lnC", "lnD", "max", "rden", "gate", "c_s", "c_max",
                                            "c_rd", "x3")}
        ln_var = {n: sem("ln_var" + n) for n in LN}
        ln_ve = {n: sem("ln_ve" + n) for n in LN}
        ln_rstd = {n: sem("ln_rstd" + n) for n in LN}
        xn_sb = {n: sem("xn_sb" + n) for n in LN}
        xnT_ps = {n: sem("xnT_ps" + n) for n in LN}
        (xin_in, cin_in, xa_in, cinc_in, ctxT_ps, ctxT_sb, kT_ps, kT_sb, xnT_sb, qT_ps, qm_sb, kbd_sb, v_ps, v_hi,
         v_lo) = map(sem, ("xin_in cin_in xa_in cinc_in ctxT_ps ctxT_sb kT_ps kT_sb xnT_sb qT_ps qm_sb kbd_sb v_ps "
                           "v_hi v_lo").split())
        (xb_sb, s_ps, s_sub, p_sb, pT_ps, p_hi, p_lo, o_ps, o_nrm, oT_ps, oT_sb, y0_ps, x1_sb) = map(
            sem, "xb_sb s_ps s_sub p_sb pT_ps p_hi p_lo o_ps o_nrm oT_ps oT_sb y0_ps x1_sb".split())
        (xh_sb, xl_sb, lg_ps, ls_sb, ge_sb, comb_sb, h_ps, th_sb, g_sb, wg_sb, acc_pool, gT_ps, gT_sb,
         y1_ps, x2_sb) = map(sem, ("xh_sb xl_sb lg_ps ls_sb ge_sb comb_sb h_ps th_sb g_sb wg_sb acc_pool "
                                   "gT_ps gT_sb y1_ps x2_sb").split())
        (cc_ps, cx_sb, kq_ps, kq_sb, s1_ps, v1_sb, nb1_sb, p1_sb, p1T_ps, p1T_sb, y2_ps, x4_sb, kr_ps, krelu_sb,
         kact_sb, thr_sb, vf_ps, u_sb, uT_ps, xo_sb) = map(
            sem, ("cc_ps cx_sb kq_ps kq_sb s1_ps v1_sb nb1_sb p1_sb p1T_ps p1T_sb y2_ps x4_sb kr_ps krelu_sb "
                  "kact_sb thr_sb vf_ps u_sb uT_ps xo_sb").split())
        xout_free = sem("xout_free")

        W1B = (L1, HB, HB + 1)
        W1CH = EXPERTS * UP // P
        ADDS = TILES * (EXPERTS - 1)
        EXP = TILES * EXPERTS
        block = stack.enter_context(nc.Block())

        def v_src(b, m):
            v = ps[SEQ * b:SEQ * b + SEQ, F0, 0:TOK].rearrange("p (n c) -> p n c", c=SEQ)
            return v.rearrange("p n (h m d) -> p n h m d", m=2, d=HD)[:, :, :, m, :]

        def v_half(buf, b, m):
            v = buf[SEQ * m:SEQ * m + SEQ, TILES * b:TILES * b + TILES, :, :, m, 0:HD]
            return v.rearrange("p t g h d -> p (t g) h d")

        def at(i, per, k):
            return i * per + k

        def wait(eng, s, value):
            if not isinstance(value, int) or value > 0:
                eng.wait_ge(s, value)

        def steps(eng, order, stage):
            first, loop, last = order

            def step(s, stages, some):
                for entry in stages:
                    name, _, lag = entry.partition("+")
                    behind = PHASES.index(PHASE.get(name[0], name[0])) + int(lag or 0)
                    once = name[0] == "W"
                    if (not 0 <= s - behind < (1 if once else GROUPS)) if some else once:
                        continue
                    n = int(name[1:]) if name[1:].isdigit() else None
                    stage(name[0] if n is not None else name, n, s - behind if behind else s)

            for s in range(LOOP_FROM):
                step(s, first, True)
            with eng.Fori(LOOP_FROM, GROUPS) as s:
                step(s, loop, False)
            for s in range(GROUPS, GROUPS + len(PHASES) - 1 + LAG):
                step(s, last, True)

        @block.sync
        def _(sp):
            def stage(name, n, i):
                if name == "F_ctx":
                    wait(sp, ctxT_ps, at(i, 1, 0))
                    sp.dma_start(cin[:, :, :], ctx_dram[:, bass.ts(i, TILES), :]).then_inc(cin_in, 16)
                    wait(sp, xn_sb["F"], at(i, TILES, 0))
                    sp.dma_start(xin[:, :, :], x_dram[:, bass.ts(i, TILES), :]).then_inc(xin_in, 16)
                if name == "W_sq":
                    for n, weight in ((WO0, L0_xattn_Wo), (WQ1, L1_xattn_Wq), (WR, L1_ffn_W_r), (WKF, L1_ffn_W_k),
                                      (WVF, L1_ffn_W_v)):
                        sp.dma_start(w_nat[:, n, :], weight).then_inc(ld_sq, 16)
                    sp.dma_start(bo0[:, :], spread(L0_xattn_bo.rearrange("(a d) -> a d", a=1), 0, P)).then_inc(ld_bo0, 16)
                if name == "W_w1":
                    sp.dma_start(w1_nat[:, :, :], L0_ffn_W1.rearrange("e (j p) d -> p (e j) d", p=P)).then_inc(ld_w1, 16)
                    sp.dma_start(wof_nat[:, :, :], L0_ffn_Wo.rearrange("d (j p) -> d j p", p=P)).then_inc(ld_small, 16)
                    sp.dma_start(wg_nat[:, :], L0_ffn_Wg).then_inc(ld_wg, 16)
                    sp.dma_start(b1_nat[:, :], L0_ffn_b1.rearrange("e (j p) -> (e j) p", p=P)).then_inc(ld_small, 16)
                    sp.dma_start(bof[:, :], spread(L0_ffn_bo.rearrange("(a d) -> a d", a=1), 0, P)).then_inc(ld_bof, 16)
                    sp.dma_start(mu[:, 0:1], L1_ffn_mu_r.rearrange("(d a) -> d a", a=1)).then_inc(ld_mu, 16)
                    sp.dma_start(mu[:, 1:2], L1_ffn_mu_k.rearrange("(d a) -> d a", a=1)).then_inc(ld_mu, 16)
                if name == "A_x":
                    wait(sp, xb_sb, at(i, 1, 0))
                    sp.dma_start(xa[:, :, :], x_dram[:, bass.ts(i, TILES), :]).then_inc(xa_in, 16)
                if name == "C_ln":
                    wait(sp, cc_ps, at(i, 1, 0))
                    sp.dma_start(cinc[:, :, :], ctx_dram[:, bass.ts(i, TILES), :]).then_inc(cinc_in, 16)

            steps(sp, SP_ORDER, stage)
            sp.wait_ge(xout_free, 16 * GROUPS + 16)

        @block.gpsimd
        def _(pool):
            pool.memset(ident[:, :], 0.0).then_inc(c_id0, 1)
            pool.wait_ge(c_id0, 1)
            pool.affine_select(out=ident[:, :], in_=ident[:, :], compare_op=ALU.not_equal, fill=1.0,
                               base=0, pattern=[[-1, P]], channel_multiplier=1).then_inc(c_ident, 1)
            pool.memset(eps_t[:, :], EPS_LN)
            pool.memset(mhalf[:, :], -0.5).then_inc(c_pow, 1)
            pool.memset(hm0[:, :, :], 0.0).then_inc(c_hm, 1)
            pool.wait_ge(c_hm, 1)
            pool.memset(hm1[:, :, :], 1.0).then_inc(c_hm, 1)
            pool.wait_ge(c_hm, 2)
            pool.affine_select(out=hm1[:, :, :], in_=hm1[:, :, :], compare_op=ALU.is_ge, fill=0.0,
                               base=0, pattern=[[-32, ROWG], [-HD, HPG]], channel_multiplier=1).then_inc(c_hm, 1)
            pool.wait_ge(c_hm, 3)
            pool.affine_select(out=hm1[:, :, :], in_=hm1[:, :, :], compare_op=ALU.is_ge, fill=0.0,
                               base=HD - 1, pattern=[[32, ROWG], [HD, HPG]], channel_multiplier=-1).then_inc(c_hm, 1)
            pool.wait_ge(c_hm, 4)
            pool.tensor_tensor(hm0[:, 0, :], hm1[:, 0, :], hm1[:, 1, :], ALU.add)
            pool.tensor_tensor(hm0[:, 1, :], hm1[:, 2, :], hm1[:, 3, :], ALU.add).then_inc(c_hm, 1)
            pool.wait_ge(c_hm, 5)
            pool.tensor_tensor(hm0[:, 2, :], hm0[:, 0, :], hm0[:, 1, :], ALU.add).then_inc(c_hm, 1)
            pool.wait_ge(c_hm, 6)
            pool.tensor_copy(headmask[:, :, :], spread(hm0[:, 2, :].unsqueeze(2), 2, SEQ)).then_inc(c_hm, 1)
            pool.wait_ge(c_hm, 7)
            pool.memset(causal[:, :], 0.0).then_inc(c_cau, 1)
            pool.wait_ge(c_cau, 1)
            pool.affine_select(out=causal[:, :], in_=causal[:, :], compare_op=ALU.is_ge, fill=NEG,
                               base=0, pattern=[[-1, P]], channel_multiplier=1).then_inc(c_cau, 1)
            pool.wait_ge(c_cau, 2)
            pool.memset(causal[SEQ:P, 0:SEQ], NEG).then_inc(c_cau, 1)
            pool.wait_ge(c_cau, 3)
            pool.wait_ge(c_pow, 1)
            pool.iota(iota_i[:, :], [[1, EXPERTS]], base=0, channel_multiplier=0).then_inc(c_iota, 1)
            pool.wait_ge(c_iota, 1)
            pool.tensor_copy(iota_e[:, :], iota_i[:, :]).then_inc(c_iota, 1)

            def stage(name, n, i):
                ln = {"F_ag": "F", "B_ag": "B", "C_ag": "C", "C_ag4": "D"}.get(name)
                if ln:
                    pool.wait_ge(ln_var[ln], at(i, 1, 1))
                    pool.tensor_tensor(vare[ln][:, :], mv[ln][:, :, 1], eps_t[:, :], ALU.add).then_inc(ln_ve[ln], 1)
                    pool.wait_ge(ln_ve[ln], at(i, 1, 1))
                    pool.tensor_tensor(rstd[ln][:, :], vare[ln][:, :], mhalf[:, :], ALU.pow).then_inc(ln_rstd[ln], 1)
                if name == "A_x":
                    pool.wait_ge(xa_in, at(i, 16, 16))
                    pool.wait_ge(ld_bo0, 16)
                    wait(pool, x1_sb, at(i, TILES, 0))
                    pool.tensor_tensor(xb[:, :, :], xa[:, :, :], spread(bo0[:, :].unsqueeze(1), 1, TILES),
                                       ALU.add).then_inc(xb_sb, 1)
                if name == "K":
                    pool.wait_ge(kT_sb, at(i, 1, 1))
                    wait(pool, s_ps, at(i, UNITS, 0))
                    pool.tensor_tensor(kbd[:, n, :, :], spread(kT[:, bass.ts(n, SEQ)].unsqueeze(1), 1, HPG),
                                       headmask[:, :, :], ALU.mult).then_inc(kbd_sb, 1)
                if name == "E":
                    t, e = divmod(n, EXPERTS)
                    if e >= 1:
                        pool.wait_ge(wg_sb, at(i, EXP, n + 1))
                        if e == 1:
                            wait(pool, gT_ps, at(i, TILES, t - 1))
                            pool.tensor_tensor(accp[:, t % 2, :], wg[:, (n - 1) % GBUF, :], wg[:, n % GBUF, :],
                                               ALU.add).then_inc(acc_pool, 1)
                        else:
                            pool.wait_ge(acc_pool, at(i, ADDS, t * (EXPERTS - 1) + e - 1))
                            pool.tensor_tensor(accp[:, t % 2, :], accp[:, t % 2, :], wg[:, n % GBUF, :],
                                               ALU.add).then_inc(acc_pool, 1)

            steps(pool, POOL_ORDER, stage)

        @block.scalar
        def _(act):
            act.dma_start(w_nat[:, WK0, :], L0_xattn_Wk).then_inc(ld_qkv, 16)
            act.dma_start(w_nat[:, WQ0, :], L0_xattn_Wq).then_inc(ld_qkv, 16)
            act.dma_start(w_nat[:, WV0, :], L0_xattn_Wv).then_inc(ld_qkv, 16)
            act.wait_ge(warm_set, 1)
            act.activation(warm[:, :], warm[:, :], ACT.Exp)

            def stage(name, n, i):
                f0, l1 = ps[:, F0, :], ps[:, L1, :]
                if name == "W_qkv":
                    act.wait_ge(wt_ps, 1)
                    act.activation(wT[:, WQ0:WV0 + 1, :], ps[:, SC, 0:3 * P], ACT.Copy).then_inc(wt_sb, 1)
                if name == "W_sq":
                    act.wait_ge(wt_ps, 2)
                    act.activation(wT[:, WVF, :], ps[:, PT, 0:P], ACT.Copy)
                    act.activation(wT[:, WO0:WKF + 1, :], ps[:, HB, :], ACT.Copy).then_inc(wt_sb, 1)
                if name == "W_small":
                    act.wait_ge(wt_ps, 3)
                    act.activation(wofT[:, :, :], ps[:, HB + 1, P:3 * P], ACT.Copy)
                    act.activation(wgh[:, :], ps[:, HB + 1, 3 * P:3 * P + EXPERTS], ACT.Copy).then_inc(wt_sb, 1)
                if name == "W":
                    act.wait_ge(w1_ps, n + 1)
                    act.activation(w1h[:, n, :], ps[:, W1B[n % 3], :], ACT.Copy).then_inc(w1_hi, 1)
                if name == "F_ctx":
                    act.wait_ge(ctxT_ps, at(i, 1, 1))
                    act.activation(ctxT[:, :], f0[:, 0:TOK], ACT.Copy).then_inc(ctxT_sb, 1)
                if name == "F_k":
                    act.wait_ge(kT_ps, at(i, 1, 1))
                    wait(act, kbd_sb, at(i, BPG, 0))
                    act.activation(kT[:, :], f0[:, TOK:2 * TOK], ACT.Copy).then_inc(kT_sb, 1)
                if name == "F_T":
                    act.wait_ge(xnT_ps["F"], at(i, 1, 1))
                    act.activation(xnT[:, :], f0[:, 0:TOK], ACT.Copy).then_inc(xnT_sb, 1)
                if name == "F_q":
                    act.wait_ge(cleared, 3)
                    act.wait_ge(qT_ps, at(i, 1, 1))
                    for g in range(ROWG):
                        rows = slice(32 * g, 32 * g + 32)
                        act.activation(qm[rows, :, g % 2, g // 2, :],
                                       ps[rows, F0, TOK:2 * TOK].rearrange("p (b t) -> p b t", b=BPG),
                                       ACT.Copy).then_inc(qm_sb, 1)
                if name == "F_v":
                    act.wait_ge(vx_ones, 2)
                    act.wait_ge(v_ps, at(i, 1, 1))
                    for b in range(2):
                        for m in range(2):
                            act.activation(v_half(vxh, b, m), v_src(b, m), ACT.Copy).then_inc(v_hi, 1)
                if name == "S":
                    act.wait_ge(s_sub, at(i, UNITS, n + 1))
                    wait(act, pT_ps, at(i, UNITS, n - 1))
                    act.activation(prob[:, n % 2, :], ssub[:, n % 2, :], ACT.Exp, scale=SCALE0).then_inc(p_sb, 1)
                if name == "T":
                    act.wait_ge(pT_ps, at(i, UNITS, n + 1))
                    wait(act, o_ps, at(i, UNITS, n - 1))
                    act.activation(ph[:, n % 2, :, :], ps[:, PT, :], ACT.Copy).then_inc(p_hi, 1)
                if name == "O":
                    act.wait_ge(oT_ps, at(i, TILES, n + 1))
                    for g in range(2):
                        for b in range(2):
                            act.activation(oT[SEQ * g:SEQ * g + SEQ, n % 2, SEQ * b:SEQ * b + SEQ],
                                           ps[SEQ * b:SEQ * b + SEQ, AO, 384 + SEQ * g:384 + SEQ * g + SEQ],
                                           ACT.Copy).then_inc(oT_sb, 1)
                if name == "B_T":
                    act.wait_ge(xnT_ps["B"], at(i, 1, 1))
                    act.activation(xh[:, :], ps[:, HB, 0:TOK], ACT.Copy).then_inc(xh_sb, 1)
                if name == "B_gate":
                    act.wait_ge(ls_sb, at(i, 1, 1))
                    act.activation(ge[:, :, :], ls[:, :, :], ACT.Exp).then_inc(ge_sb, 1)
                if name == "U":
                    act.wait_ge(h_ps, at(i, EXP, n + 1))
                    wait(act, g_sb, at(i, EXP, n + 1 - GATES))
                    act.activation(th[:, n % GATES, :], ps[:, HB + n % 2, HID:UP], ACT.Tanh,
                                   scale=0.5).then_inc(th_sb, 1)
                if name == "E":
                    t, e = divmod(n, EXPERTS)
                    act.wait_ge(comb_sb, at(i, 1, 1))
                    act.wait_ge(g_sb, at(i, EXP, n + 1))
                    mt, me = divmod(n - GBUF, EXPERTS)
                    wait(act, acc_pool, at(i, ADDS, mt * (EXPERTS - 1) + max(me, 1)))
                    act.activation(wg[:, n % GBUF, :], gb[:, n % GATES, :], ACT.Copy,
                                   scale=comb[:, t, e:e + 1]).then_inc(wg_sb, 1)
                if name == "G":
                    act.wait_ge(gT_ps, at(i, TILES, n + 1))
                    wait(act, y1_ps, at(i, TILES, n - 1))
                    act.activation(gT[:, n % 2, :, :], f0[:, 0:2 * P], ACT.Copy).then_inc(gT_sb, 1)
                if name == "C_T":
                    act.wait_ge(xnT_ps["C"], at(i, 1, 1))
                    act.activation(cx[:, :], l1, ACT.Copy).then_inc(cx_sb, 1)
                if name == "C_q":
                    act.wait_ge(kq_ps, at(i, 1, 1))
                    act.activation(kq[:, :], l1, ACT.Copy).then_inc(kq_sb, 1)
                if name == "C_s":
                    act.wait_ge(s1_ps, at(i, 1, 1))
                    act.activation(v1[:, :, :], l1[:, TOK:2 * TOK], ACT.Copy).then_inc(v1_sb, 1)
                if name == "C_p":
                    act.wait_ge(nb1_sb, at(i, 1, 1))
                    for t in range(TILES):
                        act.activation(p1[:, t, :], sm1[:, t, :], ACT.Exp, scale=SCALE1, bias=nb1[:, t:t + 1],
                                       accum_out=den1[:, t:t + 1]).then_inc(p1_sb, 1)
                if name == "C_pT":
                    act.wait_ge(p1T_ps, at(i, 1, 1))
                    act.activation(p1T[:, :, :], l1[:, 0:TOK], ACT.Copy).then_inc(p1T_sb, 1)
                if name == "C_out":
                    act.wait_ge(xo_sb, at(i, 1, 1))
                    act.dma_start(out_dram[:, bass.ts(i, TILES), :], xout[:, :, :]).then_inc(xout_free, 16)
                if name == "C_x4":
                    act.wait_ge(cleared, 4)
                    act.wait_ge(xnT_ps["D"], at(i, 1, 1))
                    act.activation(x4p[:, :, 1:SEQ + 1], l1[:, 0:TOK].rearrange("p (b t) -> p b t", b=BPG),
                                   ACT.Copy).then_inc(x4_sb, 1)
                if name == "C_kr":
                    act.wait_ge(kr_ps, at(i, 1, 1))
                    act.activation(krelu[:, :], l1[:, 0:TOK], ACT.Relu).then_inc(krelu_sb, 1)
                    act.activation(thr[:, :], l1[:, TOK:2 * TOK], ACT.Tanh, scale=0.5).then_inc(thr_sb, 1)
                if name == "C_sq":
                    act.wait_ge(krelu_sb, at(i, 1, 1))
                    act.activation(kact[:, :], krelu[:, :], ACT.Square).then_inc(kact_sb, 1)

            steps(act, ACT_ORDER, stage)

        @block.vector
        def _(dve):
            dve.memset(warm[:, :], 0.0).then_inc(warm_set, 1)
            dve.memset(vxh[:, :, :, :, :, :], 0.0).then_inc(cleared, 1)
            dve.memset(vxl[:, :, :, :, :, :], 0.0).then_inc(cleared, 1)
            dve.memset(qm[:, :, :, :, :], 0.0).then_inc(cleared, 1)
            dve.memset(x4p[:, :, 0:1], 0.0).then_inc(cleared, 1)
            dve.memset(xout[:, 0:1, 0:1], 0.0).then_inc(xout_free, 16)
            dve.wait_ge(cleared, 1)
            for m in range(2):
                dve.memset(vxh[SEQ * m:SEQ * m + SEQ, :, :, :, m, HD:HD + 1], 1.0).then_inc(vx_ones, 1)

            def stage(name, n, i):
                def moments(ln, src):
                    for t in range(TILES):
                        done = dve.bn_stats(stats[ln][:, t, :], src[:, t, :])
                    done.then_inc(own["ln" + ln], 1)

                def aggregated(ln):
                    dve.wait_ge(own["ln" + ln], at(i, 1, 1))
                    dve.memset(spare[:, LN.index(ln):LN.index(ln) + 1], 0.0)
                    for t in range(TILES):
                        done = dve.bn_aggr(mv[ln][:, t, :], stats[ln][:, t, :])
                    done.then_inc(ln_var[ln], 1)

                def normed(ln, src, w=D):
                    dve.wait_ge(ln_rstd[ln], at(i, 1, 1))
                    wait(dve, xnT_ps[ln], at(i, 1, 0))
                    for t in range(TILES):
                        dve.tensor_scalar(xn[ln][:, t, 0:w], src[:, t, 0:w], mv[ln][:, t, 0:1], rstd[ln][:, t:t + 1],
                                          ALU.subtract, ALU.mult).then_inc(xn_sb[ln], 1)

                if name == "W_adj":
                    dve.wait_ge(ld_wg, 16)
                    dve.tensor_scalar(wg_nat[:, 0:D - 1], wg_nat[:, 0:D - 1], wg_nat[:, D - 1:D], None,
                                      ALU.subtract).then_inc(wg_adj, 1)
                    dve.wait_ge(wg_adj, 1)
                    dve.memset(wg_nat[:, D - 1:D], 0.0).then_inc(wg_adj, 1)
                    dve.wait_ge(ld_w1, 16)
                    for c in range(4):
                        rows = slice(c * W1CH // 4, (c + 1) * W1CH // 4)
                        dve.tensor_tensor(w1_nat[:, rows, 0:D - 1], w1_nat[:, rows, 0:D - 1],
                                          spread(w1_nat[:, rows, D - 1:D], 2, D - 1), ALU.subtract).then_inc(w1_sub, 1)
                if name == "W_sq":
                    dve.wait_ge(ld_mu, 32)
                    dve.tensor_scalar(omu[:, :], mu[:, :], -1.0, 1.0, ALU.mult, ALU.add).then_inc(omu_s, 1)
                    dve.wait_ge(omu_s, 1)
                    dve.wait_ge(wt_sb, 2)
                    for r in range(2):
                        dve.tensor_scalar(wmix[:, r, 0, :], wT[:, WR + r, :], omu[:, r:r + 1], None, ALU.mult)
                        dve.tensor_scalar(wmix[:, r, 1, :], wT[:, WR + r, :], mu[:, r:r + 1], None,
                                          ALU.mult).then_inc(wmix_s, 1)
                if name == "W_small":
                    dve.wait_ge(w1_sub, 4)
                    dve.wait_ge(wt_sb, 3)
                    dve.tensor_copy(w1_nat[:, :, D - 1],
                                    ps[:, HB + 1, 3 * P + EXPERTS:3 * P + EXPERTS + W1CH]).then_inc(w1_adj, 1)
                    dve.tensor_tensor(wgl[:, :], ps[:, HB + 1, 3 * P:3 * P + EXPERTS], wgh[:, :],
                                      ALU.subtract).then_inc(wgl_s, 1)
                if name == "W":
                    dve.wait_ge(w1_hi, n + 1)
                    dve.tensor_tensor(w1l[:, n, :], ps[:, W1B[n % 3], :], w1h[:, n, :], ALU.subtract).then_inc(w1_lo, 1)
                if name == "F_ln":
                    dve.wait_ge(xin_in, at(i, 16, 16))
                    moments("F", xin)
                if name == "F_ag":
                    aggregated("F")
                if name == "F_T":
                    normed("F", xin)
                if name == "F_v":
                    dve.wait_ge(v_hi, at(i, VPARTS, VPARTS))
                    for b in range(2):
                        for m in range(2):
                            dve.tensor_tensor(v_half(vxl, b, m), v_src(b, m), v_half(vxh, b, m),
                                              ALU.subtract).then_inc(v_lo, 1)
                if name == "M":
                    dve.wait_ge(s_ps, at(i, UNITS, n + 1))
                    wait(dve, s_sub, at(i, UNITS, n - 1))
                    dve.tensor_reduce(mx[:, n % 2, :], ps[:, SC + n % 2, :].rearrange("p (h c) -> p h c", c=SEQ), AX.X,
                                      ALU.max).then_inc(own["max"], 1)
                if name == "S":
                    dve.wait_ge(own["max"], at(i, UNITS, n + 1))
                    wait(dve, p_sb, at(i, UNITS, n - 1))
                    dve.tensor_tensor(ssub[:, n % 2, :].rearrange("p (h c) -> p h c", c=SEQ),
                                      ps[:, SC + n % 2, :].rearrange("p (h c) -> p h c", c=SEQ),
                                      spread(mx[:, n % 2, :].unsqueeze(2), 2, SEQ), ALU.subtract).then_inc(s_sub, 1)
                if name == "T":
                    dve.wait_ge(p_hi, at(i, UNITS, n + 1))
                    dve.tensor_tensor(pl[:, n % 2, :, :], ps[:, PT, :].rearrange("p (c t) -> p c t", c=4),
                                      ph[:, n % 2, :, :], ALU.subtract).then_inc(p_lo, 1)
                if name == "R":
                    dve.wait_ge(o_ps, at(i, UNITS, 2 * n + 2))
                    wait(dve, o_nrm, at(i, 2 * TILES, 2 * n))
                    o = ps[:, AO, 0:288].rearrange("p (b g h w) -> p b g h w", b=2, g=2, w=HD + 1)
                    for g in range(2):
                        half = slice(SEQ * g, SEQ * g + SEQ)
                        done = dve.reciprocal(rden[half, :, :], o[half, :, g, :, HD])
                    done.then_inc(own["rden"], 1)
                if name == "O":
                    o = ps[:, AO, 0:288].rearrange("p (b g h w) -> p b g h w", b=2, g=2, w=HD + 1)
                    dve.wait_ge(own["rden"], at(i, TILES, n + 1))
                    wait(dve, oT_ps, at(i, TILES, n - 1))
                    for g in range(2):
                        half = slice(SEQ * g, SEQ * g + SEQ)
                        dve.tensor_tensor(onorm[half, n % 2, :].rearrange("p (b h d) -> p b h d", b=2, d=HD),
                                          o[half, :, g, :, 0:HD],
                                          spread(rden[half, :, :].unsqueeze(3), 3, HD), ALU.mult).then_inc(o_nrm, 1)
                if name == "Y":
                    dve.wait_ge(xb_sb, at(i, 1, 1))
                    dve.wait_ge(y0_ps, at(i, TILES, n + 1))
                    wait(dve, xB_sb, at(i, 1, 0))
                    dve.tensor_tensor(x1[:, n, :], ps[:, AO, 0:P], xb[:, n, :], ALU.add).then_inc(x1_sb, 1)
                if name == "B_ln":
                    dve.wait_ge(x1_sb, at(i, TILES, TILES))
                    moments("B", x1)
                if name == "B_ag":
                    aggregated("B")
                if name == "B_T":
                    wait(dve, xnT_ps["B"], at(i, 1, 0))
                    dve.memset(xn["B"][:, :, D - 1:D], 1.0)
                    normed("B", x1, D - 1)
                if name == "B_xl":
                    dve.wait_ge(xh_sb, at(i, 1, 1))
                    dve.tensor_tensor(xl[:, :], ps[:, HB, 0:TOK], xh[:, :], ALU.subtract).then_inc(xl_sb, 1)
                if name == "Q":
                    def then(ins):
                        ins.then_inc(own["gate"], 1)

                    if n == 0:
                        dve.wait_ge(lg_ps, at(i, 1, 1))
                    elif n <= GATE_STEPS:
                        dve.wait_ge(own["gate"], at(i, GATE_STEPS, n))
                    if n == 0:
                        then(dve.tensor_copy(lg[:, :, :], ps[:, HB + 1, 0:TILES * EXPERTS]))
                    if n == 1:
                        dve.memset(spare[:, 4:5], 0.0)
                        for t in range(TILES):
                            done = dve.max(top[:, t, :], lg[:, t, :])
                        then(done)
                    if n == 2:
                        dve.tensor_tensor(ls[:, :, :], lg[:, :, :], spread(top[:, :, 0:1], 2, EXPERTS),
                                          ALU.subtract).then_inc(ls_sb, 1)
                        for t in range(TILES):
                            done = dve.max_index(topi[:, t, :], top[:, t, :], lg[:, t, :])
                        then(done)
                    if n == 3:
                        then(dve.tensor_copy(topf[:, :, :], topi[:, :, 0:2]))
                    if n == 4:
                        ie = spread(iota_e[:, :].unsqueeze(1), 1, TILES)
                        dve.wait_ge(c_iota, 2)
                        dve.tensor_tensor(sel0[:, :, :], ie, spread(topf[:, :, 0:1], 2, EXPERTS), ALU.is_equal)
                        then(dve.tensor_tensor(sel1[:, :, :], ie, spread(topf[:, :, 1:2], 2, EXPERTS), ALU.is_equal))
                    if n == 5:
                        then(dve.tensor_tensor(sel0[:, :, :], sel0[:, :, :], sel1[:, :, :], ALU.add))
                    if n == 6:
                        dve.wait_ge(ge_sb, at(i, 1, 1))
                        dve.tensor_reduce(zsum[:, :], ge[:, :, :], AX.X, ALU.add)
                        then(dve.tensor_tensor(es[:, :, :], ge[:, :, :], sel0[:, :, :], ALU.mult))
                    if n == 7:
                        then(dve.tensor_reduce(ssum[:, :], es[:, :, :], AX.X, ALU.add))
                    if n == 8:
                        then(dve.scalar_tensor_tensor(gden[:, :], zsum[:, :], EPS_GATE, ssum[:, :], ALU.mult, ALU.add))
                    if n == 9:
                        then(dve.reciprocal(gden[:, :], gden[:, :]))
                    if n == 10:
                        wait(dve, wg_sb, at(i, EXP, 0))
                        for t in range(TILES):
                            done = dve.tensor_scalar(comb[:, t, :], es[:, t, :], gden[:, t:t + 1], 0.5, ALU.mult,
                                                     ALU.mult)
                        done.then_inc(comb_sb, 1)
                        dve.tensor_tensor(csum[:, :], ssum[:, :], gden[:, :], ALU.mult).then_inc(csum_sb, 1)
                    if n == 11:
                        dve.wait_ge(csum_sb, at(i, 1, 1))
                        wait(dve, x2_sb, at(i, TILES, 0))
                        dve.wait_ge(ld_bof, 16)
                        for t in range(TILES):
                            done = dve.scalar_tensor_tensor(xB[:, t, :], bof[:, :], csum[:, t:t + 1], x1[:, t, :],
                                                            ALU.mult, ALU.add)
                        done.then_inc(xB_sb, 1)
                if name == "E":
                    dve.wait_ge(th_sb, at(i, EXP, n + 1))
                    wait(dve, wg_sb, at(i, EXP, n + 1 - GATES))
                    dve.scalar_tensor_tensor(gb[:, n % GATES, :], th[:, n % GATES, :], 1.0, ps[:, HB + n % 2, 0:HID],
                                             ALU.add, ALU.mult).then_inc(g_sb, 1)
                if name == "H":
                    dve.wait_ge(y1_ps, at(i, TILES, n + 1))
                    dve.wait_ge(xB_sb, at(i, 1, 1))
                    wait(dve, own["x3"], at(i, 1, 0))
                    dve.tensor_tensor(x2[:, n, :], ps[:, F0, 2 * P:3 * P], xB[:, n, :], ALU.add).then_inc(x2_sb, 1)
                if name == "C_ln":
                    dve.wait_ge(x2_sb, at(i, TILES, TILES))
                    moments("C", x2)
                if name == "C_ag":
                    aggregated("C")
                if name == "C_T":
                    normed("C", x2)
                if name == "C_s":
                    dve.wait_ge(v1_sb, at(i, 1, 1))
                    dve.wait_ge(c_cau, 3)
                    dve.tensor_tensor(sm1[:, :, :], ps[:, L1, 0:TOK].rearrange("p (n c) -> p n c", c=P),
                                      spread(causal[:, :].unsqueeze(1), 1, TILES), ALU.add).then_inc(own["c_s"], 1)
                if name == "C_max":
                    dve.wait_ge(own["c_s"], at(i, 1, 1))
                    dve.tensor_reduce(mx1[:, :], sm1[:, :, :], AX.X, ALU.max).then_inc(own["c_max"], 1)
                if name == "C_nb":
                    dve.wait_ge(own["c_max"], at(i, 1, 1))
                    dve.tensor_scalar(nb1[:, :], mx1[:, :], -SCALE1, None, ALU.mult).then_inc(nb1_sb, 1)
                if name == "C_rd":
                    dve.wait_ge(p1_sb, at(i, TILES, TILES))
                    dve.reciprocal(rd1[:, :], den1[:, :]).then_inc(own["c_rd"], 1)
                if name == "C_y":
                    dve.wait_ge(own["c_rd"], at(i, 1, 1))
                    dve.wait_ge(y2_ps, at(i, 1, 1))
                    wait(dve, xo_sb, at(i, 1, 0))
                    for t in range(TILES):
                        done = dve.scalar_tensor_tensor(x3[:, t, :], ps[:, L1, TOK + t * P:TOK + (t + 1) * P],
                                                        rd1[:, t:t + 1], x2[:, t, :], ALU.mult, ALU.add)
                    done.then_inc(own["x3"], 1)
                if name == "C_ln4":
                    dve.wait_ge(own["x3"], at(i, 1, 1))
                    moments("D", x3)
                if name == "C_ag4":
                    aggregated("D")
                if name == "C_x4":
                    normed("D", x3)
                if name == "C_v":
                    dve.wait_ge(thr_sb, at(i, 1, 1))
                    dve.wait_ge(vf_ps, at(i, 1, 1))
                    dve.scalar_tensor_tensor(uu[:, :], thr[:, :], 1.0, ps[:, L1, 0:TOK], ALU.add,
                                             ALU.mult).then_inc(u_sb, 1)
                if name == "C_u":
                    dve.wait_ge(uT_ps, at(i, 1, 1))
                    dve.wait_ge(xout_free, at(i, 16, 16))
                    dve.scalar_tensor_tensor(xout[:, :, :], ps[:, L1, TOK:2 * TOK].rearrange("p (n d) -> p n d", d=D),
                                             0.5, x3[:, :, :], ALU.mult, ALU.add).then_inc(xo_sb, 1)

            steps(dve, DVE_ORDER, stage)

        @block.tensor
        def _(pe):
            pe.wait_ge(c_ident, 1)

            def turn(ln, i, bank, at_col):
                for t in range(TILES):
                    pe.wait_ge(xn_sb[ln], at(i, TILES, t + 1))
                    done = pe.transpose(ps[:, bank, at_col + t * P:at_col + (t + 1) * P], xn[ln][:, t, :], ident[:, :])
                done.then_inc(xnT_ps[ln], 1)

            def stage(name, n, i):
                f0, l1 = ps[:, F0, :], ps[:, L1, :]
                first = isinstance(i, int) and i == 0
                if name == "W_qkv":
                    pe.wait_ge(ld_qkv, 48)
                    for n in (WQ0, WK0, WV0):
                        done = pe.transpose(ps[:, SC, bass.ts(n - WQ0, P)], w_nat[:, n, :], ident[:, :])
                    done.then_inc(wt_ps, 1)
                if name == "W_sq":
                    pe.wait_ge(ld_sq, 16 * 5)
                    for n in (WO0, WQ1, WR, WKF):
                        pe.transpose(ps[:, HB, bass.ts(n - WO0, P)], w_nat[:, n, :], ident[:, :])
                    pe.transpose(ps[:, PT, 0:P], w_nat[:, WVF, :], ident[:, :]).then_inc(wt_ps, 1)
                if name == "W_small":
                    pe.wait_ge(ld_small, 32)
                    pe.wait_ge(wg_adj, 2)
                    for j in range(2):
                        pe.transpose(ps[:, HB + 1, (1 + j) * P:(2 + j) * P], wof_nat[:, j, :], ident[:, :])
                    pe.transpose(ps[:, HB + 1, 3 * P:3 * P + EXPERTS], wg_nat[:, :], ident[0:EXPERTS, 0:EXPERTS])
                    pe.transpose(ps[:, HB + 1, 3 * P + EXPERTS:3 * P + EXPERTS + W1CH], b1_nat[:, :],
                                 ident[0:W1CH, 0:W1CH]).then_inc(wt_ps, 1)
                if name == "W":
                    pe.wait_ge(w1_adj, 1)
                    if n == 1:
                        pe.wait_ge(wt_sb, 2)
                    if n == 2:
                        pe.wait_ge(wt_sb, 3)
                        pe.wait_ge(wgl_s, 1)
                    if n >= 3:
                        pe.wait_ge(w1_lo, n - 2)
                    for j in range(4):
                        done = pe.transpose(ps[:, W1B[n % 3], bass.ts(j, P)], w1_nat[:, 4 * n + j, :], ident[:, :])
                    done.then_inc(w1_ps, 1)
                if name == "F_ctx":
                    wait(pe, x2_sb, at(i - 2, TILES, 0))
                    wait(pe, v_lo, at(i, VPARTS, 0))
                    pe.wait_ge(cin_in, at(i, 16, 16))
                    for t in range(TILES):
                        done = pe.transpose(f0[:, bass.ts(t, P)], cin[:, t, :], ident[:, :])
                    done.then_inc(ctxT_ps, 1)
                if name == "F_k":
                    if first:
                        pe.wait_ge(wt_sb, 1)
                    pe.wait_ge(ctxT_sb, at(i, 1, 1))
                    pe.matmul(f0[:, TOK:2 * TOK], wT[:, WK0, :], ctxT[:, :], start=True, stop=True).then_inc(kT_ps, 1)
                if name == "F_T":
                    pe.wait_ge(kT_sb, at(i, 1, 1))
                    turn("F", i, F0, 0)
                if name == "F_q":
                    pe.wait_ge(xnT_sb, at(i, 1, 1))
                    pe.matmul(f0[:, TOK:2 * TOK], wT[:, WQ0, :], xnT[:, :], start=True, stop=True).then_inc(qT_ps, 1)
                if name == "F_v":
                    pe.wait_ge(qm_sb, at(i, ROWG, ROWG))
                    wait(pe, x2_sb, at(i - 2, TILES, 1))
                    if first:
                        pe.wait_ge(vx_ones, 2)
                    for n in range(TILES):
                        done = pe.matmul(f0[:, bass.ts(n, P)], ctxT[:, bass.ts(n, P)], wT[:, WV0, :], start=True,
                                         stop=True)
                    done.then_inc(v_ps, 1)
                if name == "S":
                    if first:
                        pe.wait_ge(wt_sb, 1)
                    pe.wait_ge(qm_sb, at(i, ROWG, ROWG))
                    pe.wait_ge(kbd_sb, at(i, BPG, n + 1))
                    wait(pe, s_sub, at(i, UNITS, n - 1))
                    for g in range(2):
                        done = pe.matmul(ps[:, SC + n % 2, 256 * g:256 * g + 256], qm[:, n, g, :, :], kbd[:, n, :, :],
                                         start=True, stop=True)
                    done.then_inc(s_ps, 1)
                if name == "T":
                    pe.wait_ge(p_sb, at(i, UNITS, n + 1))
                    if first and n == 0:
                        pe.wait_ge(wt_sb, 2)
                    wait(pe, p_lo, at(i, UNITS, n))
                    for c in range(4):
                        done = pe.transpose(ps[:, PT, bass.ts(c, P)], prob[:, n % 2, bass.ts(c, P)], ident[:, :])
                    done.then_inc(pT_ps, 1)
                if name == "V":
                    t, b = divmod(n, 2)
                    if n == 0:
                        pe.wait_ge(v_lo, at(i, VPARTS, VPARTS))
                    if b == 0:
                        wait(pe, x1_sb, at(i, TILES, t))
                    pe.wait_ge(p_lo, at(i, UNITS, n + 1))
                    for c in range(4):
                        o = ps[:, AO, 0:288].rearrange("p (b g h w) -> p b g h w", b=2, g=2, h=4)[:, b, :, c, :]
                        vh = vxh[:, TILES * b + t, :, c, :, :].rearrange("p g m w -> p g (m w)")
                        vl = vxl[:, TILES * b + t, :, c, :, :].rearrange("p g m w -> p g (m w)")
                        pe.matmul(o, ph[:, n % 2, c, :], vh, start=True, stop=False)
                        pe.matmul(o, ph[:, n % 2, c, :], vl, start=False, stop=False)
                        done = pe.matmul(o, pl[:, n % 2, c, :], vh, start=False, stop=True)
                    done.then_inc(o_ps, 1)
                if name == "O":
                    pe.wait_ge(o_nrm, at(i, 2 * TILES, 2 * n + 2))
                    pe.transpose(ps[:, AO, 384:512], onorm[:, n % 2, :], ident[:, :]).then_inc(oT_ps, 1)
                if name == "Y":
                    if first:
                        pe.wait_ge(wt_sb, 2)
                    pe.wait_ge(oT_sb, at(i, 4 * TILES, 4 * n + 4))
                    pe.matmul(ps[:, AO, 0:P], oT[:, n % 2, :], wT[:, WO0, :], start=True, stop=True).then_inc(y0_ps, 1)
                if name == "B_T":
                    wait(pe, g_sb, at(i, EXP, -1))
                    if first:
                        pe.wait_ge(w1_lo, EXPERTS)
                    turn("B", i, HB, 0)
                if name == "B_gate":
                    wait(pe, g_sb, at(i, EXP, 0))
                    pe.wait_ge(xh_sb, at(i, 1, 1))
                    pe.wait_ge(xl_sb, at(i, 1, 1))
                    for t in range(TILES):
                        o = ps[:, HB + 1, EXPERTS * t:EXPERTS * t + EXPERTS]
                        pe.matmul(o, xh[:, bass.ts(t, P)], wgh[:, :], start=True, stop=False)
                        pe.matmul(o, xh[:, bass.ts(t, P)], wgl[:, :], start=False, stop=False)
                        done = pe.matmul(o, xl[:, bass.ts(t, P)], wgh[:, :], start=False, stop=True)
                    done.then_inc(lg_ps, 1)
                if name == "E":
                    t, e = divmod(n, EXPERTS)
                    o = ps[:, HB + n % 2, :]
                    wait(pe, g_sb, at(i, EXP, n - 1))
                    if n == 1:
                        pe.wait_ge(own["gate"], at(i, GATE_STEPS, 1))
                    pe.matmul(o, xh[:, bass.ts(t, P)], w1h[:, e, :], start=True, stop=False)
                    pe.matmul(o, xh[:, bass.ts(t, P)], w1l[:, e, :], start=False, stop=False)
                    pe.matmul(o, xl[:, bass.ts(t, P)], w1h[:, e, :], start=False, stop=True).then_inc(h_ps, 1)
                if name == "G":
                    if not isinstance(i, int) or i + 2 < GROUPS:
                        if n == 0:
                            pe.wait_ge(qm_sb, at(i + 2, ROWG, ROWG))
                        else:
                            pe.wait_ge(v_lo, at(i + 2, VPARTS, VPARTS))
                    wait(pe, x2_sb, at(i, TILES, n))
                    pe.wait_ge(acc_pool, at(i, ADDS, (n + 1) * (EXPERTS - 1)))
                    for j in range(2):
                        done = pe.transpose(f0[:, bass.ts(j, P)], accp[:, n % 2, bass.ts(j, P)], ident[:, :])
                    done.then_inc(gT_ps, 1)
                if name == "H":
                    pe.wait_ge(gT_sb, at(i, TILES, n + 1))
                    for j in range(2):
                        done = pe.matmul(f0[:, 2 * P:3 * P], gT[:, n % 2, j, :], wofT[:, j, :],
                                         start=(j == 0), stop=(j == 1))
                    done.then_inc(y1_ps, 1)
                if name == "C_ctx":
                    wait(pe, xo_sb, at(i, 1, 0))
                    if first:
                        pe.wait_ge(w1_lo, EXPERTS)
                        pe.wait_ge(wmix_s, 2)
                    pe.wait_ge(cinc_in, at(i, 16, 16))
                    for t in range(TILES):
                        done = pe.transpose(l1[:, bass.ts(t, P)], cinc[:, t, :], ident[:, :])
                    done.then_inc(cc_ps, 1)
                if name == "C_T":
                    turn("C", i, L1, TOK)
                if name == "C_q":
                    pe.wait_ge(cx_sb, at(i, 1, 1))
                    pe.matmul(l1, wT[:, WQ1, :], cx[:, :], start=True, stop=True).then_inc(kq_ps, 1)
                if name == "C_s":
                    pe.wait_ge(kq_sb, at(i, 1, 1))
                    for t in range(TILES):
                        pe.matmul(l1[:, bass.ts(t, P)], kq[:, TOK + t * P:TOK + (t + 1) * P], kq[:, bass.ts(t, P)],
                                  start=True, stop=True)
                        done = pe.transpose(l1[:, TOK + t * P:TOK + (t + 1) * P], kq[:, bass.ts(t, P)], ident[:, :])
                    done.then_inc(s1_ps, 1)
                if name == "C_p":
                    for t in range(TILES):
                        pe.wait_ge(p1_sb, at(i, TILES, t + 1))
                        done = pe.transpose(l1[:, bass.ts(t, P)], p1[:, t, :], ident[:, :])
                    done.then_inc(p1T_ps, 1)
                if name == "C_y":
                    pe.wait_ge(p1T_sb, at(i, 1, 1))
                    for t in range(TILES):
                        done = pe.matmul(l1[:, TOK + t * P:TOK + (t + 1) * P], p1T[:, t, :], v1[:, t, :],
                                         start=True, stop=True)
                    done.then_inc(y2_ps, 1)
                if name == "C_x4":
                    turn("D", i, L1, 0)
                if name == "C_kr":
                    pe.wait_ge(x4_sb, at(i, 1, 1))
                    for r, o in ((1, l1[:, 0:TOK]), (0, l1[:, TOK:2 * TOK])):
                        pe.matmul(o, wmix[:, r, 0, :], x4p[:, :, 0:SEQ], start=True, stop=False)
                        done = pe.matmul(o, wmix[:, r, 1, :], x4p[:, :, 1:SEQ + 1], start=False, stop=True)
                    done.then_inc(kr_ps, 1)
                if name == "C_v":
                    pe.wait_ge(kact_sb, at(i, 1, 1))
                    pe.matmul(l1[:, 0:TOK], wT[:, WVF, :], kact[:, :], start=True, stop=True).then_inc(vf_ps, 1)
                if name == "C_u":
                    pe.wait_ge(u_sb, at(i, 1, 1))
                    for t in range(TILES):
                        done = pe.transpose(l1[:, TOK + t * P:TOK + (t + 1) * P], uu[:, bass.ts(t, P)], ident[:, :])
                    done.then_inc(uT_ps, 1)

            steps(pe, PE_ORDER, stage)
    return nc


_INS = ['x', 'ctx_1024', 'L0_xattn_Wq', 'L0_xattn_Wk', 'L0_xattn_Wv', 'L0_xattn_Wo', 'L0_xattn_bo', 'L0_ffn_Wg',
        'L0_ffn_W1', 'L0_ffn_b1', 'L0_ffn_Wo', 'L0_ffn_bo', 'L1_xattn_Wq', 'L1_ffn_W_r', 'L1_ffn_W_k', 'L1_ffn_W_v',
        'L1_ffn_mu_r', 'L1_ffn_mu_k']


def kernel(**inputs):
    import numpy as _np
    import concourse.bacc as _bacc
    from concourse.bass_utils import run_bass_kernel_spmd as _run

    nc = _bacc.Bacc("TRN2", target_bir_lowering=False, num_devices=1)
    arrays, args = {}, []
    for name in _INS:
        a = _np.ascontiguousarray(inputs[name])
        arrays[f"in_{name}"] = a
        args.append(nc.dram_tensor(f"in_{name}", a.shape, mybir.dt.from_np(a.dtype), kind="ExternalInput").ap())
    args.append(nc.dram_tensor("out_x", (BATCH, SEQ, D), F32, kind="ExternalOutput").ap())
    build(nc, *args)
    r = _run(nc, [arrays], core_ids=[0])
    return r.results[0]["out_x"]
```
